# Optimizing a Trainium2 kernel written in Bass

```python
import numpy as np
import jax
import jax.numpy as jnp

def _softmax(x, axis=-1):
    return jax.nn.softmax(x, axis=axis)

def _gelu(x):
    return jax.nn.gelu(x, approximate=True)

def _silu(x):
    return jax.nn.silu(x)

def _sigmoid(x):
    return jax.nn.sigmoid(x)

def _layernorm(x, axis=-1, eps=1e-05):
    m = jnp.mean(x, axis=axis, keepdims=True)
    v = jnp.var(x, axis=axis, keepdims=True)
    return (x - m) / jnp.sqrt(v + eps)

def _scatter_add(tgt, idx, src, axis=0):
    return tgt.at[idx].add(src)

def _segment_sum(src, seg, n):
    return jax.ops.segment_sum(src, seg, n)
kernel_name = 'mk_sandwich_d1_jaxref_r4_da72ca'

def setup_inputs(seed: int=0):
    np.random.seed(seed)
    _w = jnp.asarray

    def _L0_attn_setup():
        import jax, jax.numpy as jnp
        import numpy as np
        DIM = 256
        DIM_HEAD = 64
        HEADS = DIM // DIM_HEAD
        B, N = (2, 512)
        LN_EPS = 1e-05
        RMS_EPS = 1e-08

        def _rmsnorm(x, gamma):
            d = x.shape[-1]
            norm = jnp.linalg.norm(x, axis=-1, keepdims=True) * d ** (-0.5)
            return x / jnp.maximum(norm, RMS_EPS) * gamma

        def _layernorm(x, gamma, beta):
            mu = jnp.mean(x, axis=-1, keepdims=True)
            var = jnp.var(x, axis=-1, keepdims=True)
            return (x - mu) * jax.lax.rsqrt(var + LN_EPS) * gamma + beta
        key = jax.random.key(seed)
        ks = jax.random.split(key, 8)
        s = DIM ** (-0.5)
        return {'x': jax.random.normal(ks[0], (B, N, DIM), dtype=jnp.float32), 'ln_gamma': jnp.ones((DIM,), jnp.float32), 'ln_beta': jnp.zeros((DIM,), jnp.float32), 'q_gamma': jnp.ones((DIM_HEAD,), jnp.float32), 'k_gamma': jnp.ones((DIM_HEAD,), jnp.float32), 'w_q': jax.random.normal(ks[1], (DIM, DIM), jnp.float32) * s, 'w_k': jax.random.normal(ks[2], (DIM, DIM), jnp.float32) * s, 'w_v': jax.random.normal(ks[3], (DIM, DIM), jnp.float32) * s, 'w_o': jax.random.normal(ks[4], (DIM, DIM), jnp.float32) * s, 'b_o': jnp.zeros((DIM,), jnp.float32)}
    _L0_attn_in = _L0_attn_setup()

    def _L0_ffn_setup():
        import jax, jax.numpy as jnp
        import numpy as np
        B, S, H, E = (2, 2048, 256, 8)
        SCALE = 0.5
        key = jax.random.key(seed)
        k1, k2 = jax.random.split(key)
        x = jax.random.normal(k1, (B, S, H), dtype=jnp.float32)
        gate_w = jax.random.normal(k2, (E, H), dtype=jnp.float32) * 0.02
        coeff = SCALE * (1.0 + 0.05 * jnp.arange(E, dtype=jnp.float32))
        expert_w = coeff[:, None, None] * jnp.eye(H, dtype=jnp.float32)
        return {'x': x, 'gate_w': gate_w, 'expert_w': expert_w}
    _L0_ffn_in = _L0_ffn_setup()
    _d = {'L0_attn_x': _L0_attn_in['x'], 'L0_attn_ln_gamma': _L0_attn_in['ln_gamma'], 'L0_attn_ln_beta': _L0_attn_in['ln_beta'], 'L0_attn_q_gamma': _L0_attn_in['q_gamma'], 'L0_attn_k_gamma': _L0_attn_in['k_gamma'], 'L0_attn_w_q': _L0_attn_in['w_q'], 'L0_attn_w_k': _L0_attn_in['w_k'], 'L0_attn_w_v': _L0_attn_in['w_v'], 'L0_attn_w_o': _L0_attn_in['w_o'], 'L0_attn_b_o': _L0_attn_in['b_o'], 'L0_ffn_gate_w': _L0_ffn_in['gate_w'], 'L0_ffn_expert_w': _L0_ffn_in['expert_w']}
    _x0 = _d['L0_attn_x']
    _d['L0_attn_x'] = jax.random.normal(jax.random.fold_in(jax.random.key(seed), 1), (2, 2048, 256), dtype=_x0.dtype)
    del _x0
    return _d

def reference(L0_attn_x, L0_attn_ln_gamma, L0_attn_ln_beta, L0_attn_q_gamma, L0_attn_k_gamma, L0_attn_w_q, L0_attn_w_k, L0_attn_w_v, L0_attn_w_o, L0_attn_b_o, L0_ffn_gate_w, L0_ffn_expert_w):

    def _L0_attn_ref(x, ln_gamma, ln_beta, q_gamma, k_gamma, w_q, w_k, w_v, w_o, b_o):
        import jax, jax.numpy as jnp
        import numpy as np
        DIM = 256
        DIM_HEAD = 64
        HEADS = DIM // DIM_HEAD
        B, N = (2, 512)
        LN_EPS = 1e-05
        RMS_EPS = 1e-08

        def _rmsnorm(x, gamma):
            d = x.shape[-1]
            norm = jnp.linalg.norm(x, axis=-1, keepdims=True) * d ** (-0.5)
            return x / jnp.maximum(norm, RMS_EPS) * gamma

        def _layernorm(x, gamma, beta):
            mu = jnp.mean(x, axis=-1, keepdims=True)
            var = jnp.var(x, axis=-1, keepdims=True)
            return (x - mu) * jax.lax.rsqrt(var + LN_EPS) * gamma + beta
        h, dh = (HEADS, DIM_HEAD)
        xn = _layernorm(x, ln_gamma, ln_beta)

        def proj(w):
            y = xn @ w.T
            b, n, _ = y.shape
            return y.reshape(b, n, h, dh).transpose(0, 2, 1, 3)
        q = proj(w_q)
        k = proj(w_k)
        v = proj(w_v)
        qn = _rmsnorm(q, q_gamma) * dh ** (-0.5)
        kn = _rmsnorm(k, k_gamma)
        sim = jnp.einsum('bhid,bhjd->bhij', qn, kn)
        attn = jax.nn.softmax(sim, axis=-1)
        out = jnp.einsum('bhij,bhjd->bhid', attn, v)
        b, _, n, _ = out.shape
        out = out.transpose(0, 2, 1, 3).reshape(b, n, h * dh)
        return out @ w_o.T + b_o

    def _L0_ffn_ref(x, gate_w, expert_w):
        import jax, jax.numpy as jnp
        import numpy as np
        B, S, H, E = (2, 2048, 256, 8)
        SCALE = 0.5
        scores = jnp.einsum('bsh,eh->bse', x, gate_w)
        chosen = jnp.argmax(scores, axis=-1)
        onehot = jax.nn.one_hot(chosen, gate_w.shape[0], dtype=x.dtype)
        expert_out = jnp.einsum('bsh,efh->bsef', x, expert_w)
        return x + jnp.einsum('bsef,bse->bsf', expert_out, onehot)
    x = L0_attn_x
    x = x + _layernorm(_L0_attn_ref(_layernorm(x, axis=-1), L0_attn_ln_gamma, L0_attn_ln_beta, L0_attn_q_gamma, L0_attn_k_gamma, L0_attn_w_q, L0_attn_w_k, L0_attn_w_v, L0_attn_w_o, L0_attn_b_o), axis=-1)
    x = x + _layernorm(_L0_ffn_ref(_layernorm(x, axis=-1), L0_ffn_gate_w, L0_ffn_expert_w), axis=-1)
    return x

_drawn_inputs = setup_inputs


def setup_inputs(seed=0):
    import zlib

    import numpy as np

    out = dict(_drawn_inputs(seed))
    spreads = {'L0_attn_ln_gamma': (1.0, 0.2),
     'L0_attn_ln_beta': (0.0, 0.1),
     'L0_attn_q_gamma': (1.0, 0.2),
     'L0_attn_k_gamma': (1.0, 0.2),
     'L0_attn_b_o': (0.0, 0.1)}
    factors = {}
    for name, (base, spread) in spreads.items():
        noise = np.random.default_rng([zlib.crc32(name.encode()), seed]).standard_normal(out[name].shape)
        drawn = base * np.exp(spread * noise) if base else spread * noise
        out[name] = jnp.asarray(drawn.astype(out[name].dtype))
    for name, factor in factors.items():
        out[name] = (out[name] * factor).astype(out[name].dtype)
    return out
```

```python
import math
from contextlib import ExitStack

import concourse.bass as bass
from concourse import mybir


def build(nc, x, wqkvT, woT, weT, wgT, ln_gamma, ln_beta, q_gamma, k_gamma, b_o, out):
    f32, f32r, f16, u32 = mybir.dt.float32, mybir.dt.float32r, mybir.dt.float16, mybir.dt.uint32
    ALU, ACT, AX = mybir.AluOpType, mybir.ActivationFunctionType, mybir.AxisListType
    P = 128
    NB, N, D = x.shape
    DH = q_gamma.shape[0]
    H = D // DH
    KH = D // P
    NE = wgT.shape[1]
    NT = N // P
    TG = 4
    NG = NT // TG
    QB = 1024
    NQB = N // QB
    QT = QB // P
    BANK = 512
    STEPS = NQB * NT
    LAG = 3
    NEF, NEP = 2, 4
    VW = DH + 1 + DH
    VS = VW + 1
    XR = 4
    LN_EPS, RMS_EPS = 1e-5, 1e-8
    KSCALE = 32.0
    QMAX = 512.0
    TOP = 10.5

    nc.disable_value_cache = True
    with ExitStack() as ctx:
        def sb(name, shape, dt):
            return ctx.enter_context(nc.sbuf_tensor(name, shape, dt))

        def sem(name):
            return ctx.enter_context(nc.semaphore(name))

        x_all = sb("x_all", [P, NB * NT, D], f32)
        wqkv_h, wqkv_l = (sb(n, [P, KH, 3 * D], f32r) for n in ("wqkv_h", "wqkv_l"))
        wo_h, wo_l = (sb(n, [P, KH, D], f32r) for n in ("wo_h", "wo_l"))
        we_h, we_l = (sb(n, [P, KH, NE * D], f32r) for n in ("we_h", "we_l"))
        wg_h, wg_l = (sb(n, [P, KH, NE], f32r) for n in ("wg_h", "wg_l"))
        q_T = sb("q_T", [P, H * N], f16)
        k_T = sb("k_T", [P, 2, H * N], f16)
        v_mm = sb("v_mm", [P, NT * H, VS], f16)
        attn = sb("attn", [P, H * NQB * QT, DH], f32)
        lsum = sb("lsum", [P, H * NQB * QT], f32)
        e_f = sb("e_f", [P, NEF, QB], f32)
        e_h, e_l = (sb(n, [P, NEP, QB], f16) for n in ("e_h", "e_l"))
        ov_l = sb("ov_l", [P, QT, DH], f32)
        y_h, y_l = (sb(n, [P, KH, TG * P], f32r) for n in ("y_h", "y_l"))
        e_f32 = e_f[:, :, :].rearrange("p s n -> p (s n)")
        y_f = e_f32[:, 0:KH * TG * P].rearrange("p (k n) -> p k n", k=KH)
        sq = e_f32[:, 1024:1024 + 2 * D]
        qk_n = e_f32[:, 1536:1536 + 2 * D]
        e_h32 = e_h[:, :, :].rearrange("p s n -> p (s n)")
        xhat = e_h32[:, 0:2 * TG * D].bitcast(f32).rearrange("p (t d) -> p t d", d=D)
        qk_s = e_h32[:, 2048:2048 + 6 * H * DH].rearrange("p (h c) -> p h c", h=2 * H)
        q_sq = e_h32[:, 3584:3584 + 2 * D].bitcast(f32)
        ident = sb("ident", [P, P], f32)
        ident16 = sb("ident16", [P, P], f16)
        ones = sb("ones", [P, P], f32)
        gam, bet = (sb(n, [P, KH], f32) for n in ("gam", "bet"))
        gam_row, bet_row, bo_row = (sb(n, [P, D], f32) for n in ("gam_row", "bet_row", "bo_row"))
        qg_row, kg_row = (sb(n, [P, DH], f32) for n in ("qg_row", "kg_row"))
        gq = sb("gq", [P, DH], f32)
        c_ = sb("c_", [P, 24], f32)
        part = sb("part", [P, 4], f32)
        st = sb("st", [P, TG, 6], f32)
        mv = sb("mv", [P, TG, 2], f32)
        var, sd, rs = (sb(n, [P, TG], f32) for n in ("var", "sd", "rs"))
        ss, nr, nm, rn = (sb(n, [P, 2 * H], f32) for n in ("ss", "nr", "nm", "rn"))
        rcol = sb("rcol", [P, 2 * H], f32)
        qn2 = sb("qn2", [P, NT, H], f32)
        qmx = sb("qmx", [P, H], f32)
        qmT = sb("qmT", [H, 1], f32)
        qmD = sb("qmD", [H, H], f32)
        nbias = sb("nbias", [P, H], f32)
        rl = sb("rl", [P, H, TG], f32)
        gs = sb("gs", [P, TG, NE], f32)
        gm = sb("gm", [P, TG], f32)
        hot = sb("hot", [P, TG, NE], f32)
        rank = sb("rank", [P, NE], f32)
        st2 = sb("st2", [P, 6], f32)
        mv2 = sb("mv2", [P, 2], f32)
        sc2 = sb("sc2", [P, 4], f32)
        f_a, f_b = (sb(n, [P, D], f32) for n in ("f_a", "f_b"))

        banks = ctx.enter_context(nc.psum_tensor("banks", [P, 8 * BANK], f32))

        def bank(i, n=1):
            return banks[:, i * BANK:(i + n) * BANK]

        ps_S = [bank(0, 2), bank(2, 2)]
        ps_O = bank(4, 4).rearrange("p (b c) -> p b c", c=BANK)[:, :, 0:2 * VW].rearrange(
            "p b (q c) -> p b q c", c=VW)
        ps_T = bank(0, 2).rearrange("p (k c) -> p k c", k=KH)
        ps_QK = [bank(2), bank(3)]
        ps_V = [bank(4)[:, 0:D], bank(5)[:, 0:D]]
        ps_TQ = bank(6).bitcast(f16)[:, 0:H * P]
        ps_TK = bank(7).bitcast(f16)[:, 0:2 * H * P]
        ps_X = [bank(2 + i) for i in range(XR)]
        ps_Y = [bank(6), bank(7)]
        ps_G = bank(6)[:, 0:TG * NE]

        raw_we = k_T[:, :, :].rearrange("p a n -> p (a n)").bitcast(f32)[:, 0:KH * NE * D].rearrange(
            "p (k n) -> p k n", k=KH)
        raw_q = q_T[:, :].bitcast(f32)
        raw_wqkv = raw_q[:, 0:KH * 3 * D].rearrange("p (k n) -> p k n", k=KH)
        raw_wo = raw_q[:, KH * 3 * D:KH * 4 * D].rearrange("p (k n) -> p k n", k=KH)
        raw_wg = sb("raw_wg", [P, KH, NE], f32)

        CQ, CESC, CV, CIV = (c_[:, i:i + 1] for i in range(4))
        tmp = [c_[:, i:i + 1] for i in range(4, 16)]

        owned = {}

        def sems(owner, names):
            made = [sem("s_" + n) for n in names.split()]
            owned.setdefault(owner, []).extend(made)
            return made

        def wait(eng, s, value):
            eng.wait_ge(s, value + any(s is m for group in owned.values() for m in group))

        def start_at_one(eng, owner):
            for s in owned.get(owner, []):
                eng.sem_inc(s, 1)

        s_x, s_small, s_wq, s_we, s_out = (sem("s_" + n) for n in "x small wq we out".split())
        s_id, s_rank, s_ones, s_qg, s_q2 = sems("pool", "id rank ones qg q2")
        s_prep, s_const, s_ws = sems("dve", "prep const ws")
        s_dve, s_var, s_xh, s_ys, s_ss, s_qkn, s_lo, s_vl, s_qe, s_qs, s_mxD, s_nb = sems(
            "dve", "dve var xh ys ss qkn lo vl qe qs mxD nb")
        s_held, = sems("dve", "held")
        s_EhD, s_El, s_Oev = sems("dve", "EhD El Oev")
        s_c, s_at, s_al, s_var3, s_xn, s_nl, s_Xr, s_var5, s_fin = sems("dve", "c at al var3 xn nl Xr var5 fin")
        s_prepA, s_wh, s_sd, s_y, s_sq, s_vh, s_nr, s_hi, s_ke, s_mx = sems("act", "prepA wh sd y sq vh nr hi ke mx")
        s_E, s_EhA, s_OL, s_ah, s_sd3, s_nh, s_sd5 = sems("act", "E EhA OL ah sd3 nh sd5")
        s_prepP, s_T, s_P, s_T2, s_mxT, s_mxB = sems("pe", "prepP T P T2 mxT mxB")
        s_S, s_PV, s_T3, s_Y, s_T4, s_G, s_X = sems("pe", "S PV T3 Y T4 G X")

        x_d = x.rearrange("b (t p) d -> p (b t) d", p=P)
        out_d = out.rearrange("b (t p) d -> p (b t) d", p=P)

        def spread(ap, axis, n):
            ap = ap.unsqueeze(axis)
            shape = list(ap.shape)
            shape[axis] = n
            return ap.to_broadcast(shape)

        ACT_H = set(range(0, STEPS, 2))

        block = ctx.enter_context(nc.Block())

        @block.sync
        def _(sp):
            sp.dma_start(x_all[:, 0:TG, :], x_d[:, 0:TG, :]).then_inc(s_x, 16)
            sp.dma_start(raw_wqkv, wqkvT.rearrange("(k p) n -> p k n", p=P)).then_inc(s_wq, 16)
            sp.dma_start(raw_wo, woT.rearrange("(k p) n -> p k n", p=P)).then_inc(s_wq, 16)
            with sp.Fori(1, NB * NG) as g:
                wait(sp, s_x, g * 16)
                sp.dma_start(x_all[:, bass.ds(g * TG, TG), :], x_d[:, bass.ds(g * TG, TG), :]).then_inc(s_x, 16)
            with sp.Fori(0, NB) as b:
                with sp.Fori(0, NG) as g:
                    wait(sp, s_fin, (b * NG + g) * TG + TG)
                    sp.dma_start(out_d[:, bass.ds((b * NG + g) * TG, TG), :],
                                 x_all[:, bass.ds((b * NG + g) * TG, TG), :]).then_inc(s_out, 16)
            wait(sp, s_out, NB * NG * 16)

        @block.gpsimd
        def _(pool):
            start_at_one(pool, "pool")
            for m in (ident, ident16):
                pool.memset(m[:, :], 0.0).then_inc(s_id, 1)
            pool.memset(ones[:, :], 1.0).then_inc(s_ones, 1)
            for e in range(NE):
                pool.memset(rank[:, e:e + 1], float(NE - e)).then_inc(s_rank, 1)
            for i in range(2 * H):
                pool.memset(rcol[:, i:i + 1], 1.0 if i < H else 1.0 / KSCALE).then_inc(s_rank, 1)
            pool.memset(v_mm[:, :, DH:DH + 1], 1.0).then_inc(s_ones, 1)
            wait(pool, s_id, 2)
            for m in (ident, ident16):
                pool.affine_select(out=m[:, :], in_=m[:, :], compare_op=ALU.not_equal, fill=1.0, base=0,
                                   pattern=[[-1, P]], channel_multiplier=1).then_inc(s_id, 1)
            wait(pool, s_const, 1)
            with pool.Fori(0, NB * NG) as g:
                for t in range(TG):
                    n = g * TG + t
                    qv = qk_n[:, 0:D].rearrange("p (h d) -> p h d", h=H)
                    wait(pool, s_qkn, n + 1)
                    pool.tensor_tensor(qv, qv, spread(gq[:, :], 1, H), ALU.mult).then_inc(s_qg, 1)
                    wait(pool, s_qg, n + 1)
                    wait(pool, s_qs, n)
                    pool.tensor_tensor(q_sq[:, :], qk_n[:, 0:D], qk_n[:, 0:D], ALU.mult).then_inc(s_q2, 1)

        @block.scalar
        def _(act):
            start_at_one(act, "act")
            for col, src in ((gam, ln_gamma), (bet, ln_beta)):
                for k in range(KH):
                    act.dma_start(col[:, k:k + 1], src[k * P:(k + 1) * P].rearrange("(p o) -> p o", o=1)).then_inc(s_small, 16)
            for dst, src in ((gam_row, ln_gamma), (bet_row, ln_beta), (bo_row, b_o), (qg_row, q_gamma), (kg_row, k_gamma)):
                act.dma_start(dst[:, :], src.partition_broadcast(P)).then_inc(s_small, 16)
            act.dma_start(raw_wg[:, :, :], wgT.rearrange("(k p) n -> p k n", p=P)).then_inc(s_small, 16)
            act.dma_start(raw_we, weT.rearrange("(k p) n -> p k n", p=P)).then_inc(s_we, 16)
            wait(act, s_wq, 32)
            act.activation(wqkv_h[:, :, :], raw_wqkv, ACT.Copy).then_inc(s_wh, 1)
            act.activation(wo_h[:, :, :], raw_wo, ACT.Copy).then_inc(s_wh, 1)
            wait(act, s_small, 160)
            act.activation(wg_h[:, :, :], raw_wg[:, :, :], ACT.Copy).then_inc(s_wh, 1)
            act.activation(xhat[:, 0:KH, :], raw_wqkv[:, :, 2 * D:3 * D], ACT.Square, accum_out=part[:, 0:1]).then_inc(s_prepA, 1)
            act.activation(sq[:, 0:D], gam_row[:, :], ACT.Square, accum_out=part[:, 1:2]).then_inc(s_prepA, 1)
            act.activation(sq[:, D:2 * D], bet_row[:, :], ACT.Square, accum_out=part[:, 2:3]).then_inc(s_prepA, 1)
            wait(act, s_we, 16)
            act.activation(we_h[:, :, :], raw_we, ACT.Copy).then_inc(s_wh, 1)
            wait(act, s_prep, 6)
            act.activation(tmp[7], tmp[6], ACT.Sqrt).then_inc(s_prepA, 1)

            def ln_root(g):
                wait(act, s_var, g + 1)
                act.activation(sd[:, :], var[:, :], ACT.Sqrt).then_inc(s_sd, 1)

            def front_y(g):
                wait(act, s_T, g + 1)
                wait(act, s_ys, g)
                for k in range(KH):
                    act.activation(y_f[:, k, :], ps_T[:, k, :], ACT.Identity, bias=bet[:, k:k + 1],
                                   scale=gam[:, k:k + 1]).then_inc(s_y, 1)

            def tile_a(g, t):
                n = g * TG + t
                wait(act, s_P, n + 1)
                wait(act, s_ss, n)
                act.activation(sq[:, :], ps_QK[t % 2], ACT.Square).then_inc(s_sq, 1)
                act.activation(v_slot(n, g, t, 0), ps_V[t % 2].rearrange("p (h d) -> p h d", h=H), ACT.Copy,
                               scale=CV).then_inc(s_vh, 1)
                wait(act, s_ss, n + 1)
                act.activation(nr[:, :], ss[:, :], ACT.Sqrt, scale=1.0 / DH).then_inc(s_nr, 1)
                wait(act, s_qg, n + 1)
                wait(act, s_T2, n)
                act.activation(qk_s[:, :, 0:DH], qk_n[:, :].rearrange("p (h d) -> p h d", d=DH), ACT.Copy).then_inc(s_hi, 1)
                act.activation(qk_s[:, H:, 2 * DH:], qk_n[:, D:].rearrange("p (h d) -> p h d", d=DH), ACT.Copy).then_inc(s_hi, 1)
                wait(act, s_T2, n + 1)
                act.activation(k_T[:, :, :].rearrange("p a (h n) -> p h a n", h=H)[:, :, :, bass.ds(col(g, t), P)],
                               ps_TK.rearrange("p (h a n) -> p h a n", h=H, a=2), ACT.Copy).then_inc(s_ke, 1)

            with act.Fori(0, NB) as b:
                with act.Fori(0, NG) as gi:
                    g = b * NG + gi

                    def v_slot(n, g, t, low):
                        return v_mm[:, bass.ds(gi * (TG * H) + t * H, H), (DH + 1) * low:(DH + 1) * low + DH]

                    def col(g, t):
                        return gi * (TG * P) + t * P

                    ln_root(g)
                    front_y(g)
                    for t in range(TG):
                        tile_a(g, t)
                wait(act, s_mxB, b + 1)
                act.activation(nm[:, 0:H], bank(0)[:, 0:H], ACT.Sqrt).then_inc(s_mx, 1)
                wait(act, s_nb, 2 * b + 2)

                def exp_step(hh, h, k):
                    s = hh * STEPS + k
                    wait(act, s_S, s + 1)
                    if not (isinstance(h, int) and k < NEF):
                        wait(act, s_El, s - NEF + 1)
                    act.activation(e_f[:, k % NEF, :], ps_S[k % 2], ACT.Exp, bias=bias_of(h), scale=CESC).then_inc(s_E, 1)
                    if k in ACT_H:
                        if not (isinstance(h, int) and k < NEP):
                            wait(act, s_PV, s - NEP + 1)
                        act.activation(e_h[:, k % NEP, :], ps_S[k % 2], ACT.Exp, bias=bias_of(h), scale=CESC).then_inc(s_EhA, 1)

                def low_out(unit):
                    wait(act, s_PV, unit * NT + NT)
                    wait(act, s_Oev, 2 * unit)
                    act.activation(ov_l[:, :, :].rearrange("p (b q) d -> p b q d", q=2), ps_O[:, :, :, DH + 1:],
                                   ACT.Copy).then_inc(s_OL, 1)

                def bias_of(h):
                    return nbias[:, h:h + 1] if isinstance(h, int) else nbias[:, bass.ds(h, 1)]

                def head_act(b, h):
                    hh = b * H + h
                    for k in range(STEPS):
                        exp_step(hh, h, k)
                        if k % NT == LAG - 1 and not (isinstance(h, int) and k < NT):
                            low_out(hh * NQB + k // NT - 1)

                head_act(b, 0)
                with act.Fori(1, H) as h:
                    head_act(b, h)
                low_out(b * H * NQB + H * NQB - 1)

                def c_part(g, part_):
                    if part_ == 0:
                        wait(act, s_T3, g + 1)
                        wait(act, s_X, g * TG * XR)
                        act.activation(y_h[:, :, :], ps_T, ACT.Copy).then_inc(s_ah, 1)
                    elif part_ == 2:
                        wait(act, s_var3, 2 * g + 1)
                        act.activation(sd[:, :], var[:, :], ACT.Sqrt).then_inc(s_sd3, 1)
                        wait(act, s_var3, 2 * g + 2)
                        act.activation(sd[:, :], var[:, :], ACT.Sqrt).then_inc(s_sd3, 1)
                        wait(act, s_T4, g + 1)
                        act.activation(y_h[:, :, :], ps_T, ACT.Copy).then_inc(s_nh, 1)

                with act.Fori(0, NG) as gi:
                    g = b * NG + gi
                    for p_ in range(4):
                        c_part(g, p_)
                    for t in range(TG):
                        wait(act, s_var5, g * TG + t + 1)
                        act.activation(sc2[:, 1:2], sc2[:, 0:1], ACT.Sqrt).then_inc(s_sd5, 1)

        @block.vector
        def _(dve):
            start_at_one(dve, "dve")
            wait(dve, s_prepP, 1)
            wait(dve, s_prepA, 3)
            dve.tensor_scalar(tmp[4], part[:, 1:2], float(D), None, ALU.mult).then_inc(s_prep, 1)
            wait(dve, s_prep, 1)
            dve.tensor_tensor(tmp[5], tmp[4], part[:, 2:3], ALU.add).then_inc(s_prep, 1)
            wait(dve, s_prep, 2)
            dve.tensor_scalar(tmp[8], bank(0)[:, 0:1], 2.0, None, ALU.mult).then_inc(s_prep, 1)
            wait(dve, s_prep, 3)
            dve.tensor_tensor(tmp[9], tmp[5], tmp[8], ALU.mult).then_inc(s_prep, 1)
            wait(dve, s_prep, 4)
            dve.tensor_scalar(tmp[10], tmp[9], 1e-30, None, ALU.max).then_inc(s_prep, 1)
            wait(dve, s_prep, 5)
            dve.tensor_scalar(tmp[6], tmp[10], 2.0 ** -28, None, ALU.mult).then_inc(s_prep, 1)
            wait(dve, s_small, 160)
            dve.tensor_tensor(gq[:, :], qg_row[:, :], kg_row[:, :], ALU.mult).then_inc(s_prep, 1)
            wait(dve, s_prep, 7)
            dve.tensor_reduce(tmp[0], gq[:, :], AX.X, ALU.max, apply_absolute_value=True).then_inc(s_prep, 1)
            wait(dve, s_prep, 8)
            dve.tensor_scalar(tmp[1], tmp[0], 1e-30, 1.0 / QMAX, ALU.max, ALU.mult).then_inc(s_prep, 1)
            wait(dve, s_prep, 9)
            dve.reciprocal(tmp[2], tmp[1]).then_inc(s_prep, 1)
            wait(dve, s_prepA, 4)
            dve.reciprocal(tmp[11], tmp[7]).then_inc(s_prep, 1)
            wait(dve, s_prep, 11)
            dve.tensor_scalar(CQ.bitcast(u32), tmp[2].bitcast(u32), 0x7F800000, None, ALU.bitwise_and).then_inc(s_prep, 1)
            dve.tensor_scalar(CV.bitcast(u32), tmp[11].bitcast(u32), 0x7F800000, None, ALU.bitwise_and).then_inc(s_prep, 1)
            wait(dve, s_prep, 13)
            dve.reciprocal(CIV, CV).then_inc(s_prep, 1)
            dve.reciprocal(tmp[3], CQ).then_inc(s_prep, 1)
            wait(dve, s_prep, 15)
            dve.tensor_scalar(CESC, tmp[3], 1.0 / (KSCALE * math.sqrt(DH)), None, ALU.mult).then_inc(s_prep, 1)
            wait(dve, s_prep, 16)
            dve.tensor_scalar(gq[:, :], gq[:, :], CQ, None, ALU.mult).then_inc(s_const, 1)
            for i, (w, hi, lo) in enumerate(((raw_wqkv, wqkv_h, wqkv_l), (raw_wo, wo_h, wo_l), (raw_wg[:, :, :], wg_h, wg_l), (raw_we, we_h, we_l))):
                wait(dve, s_wh, i + 1)
                dve.tensor_tensor(lo[:, :, :], w, hi[:, :, :].bitcast(f32), ALU.subtract).then_inc(s_ws, 1)

            chain = [0, None, 0]

            def link(ins):
                ins.then_inc(s_dve, 1)
                chain[0] += 1

            def follow():
                wait(dve, s_dve, chain[1] + chain[0])

            def stats(g, src):
                for t in range(TG):
                    dve.bn_stats(st[:, t, :], src(t)).then_inc(s_dve, 1)
                    chain[0] += 1
                follow()
                dve.sem_inc(s_held, 1)
                for t in range(TG):
                    link(dve.bn_aggr(mv[:, t, :], st[:, t, :]))
                follow()

            def front_ln(g):
                wait(dve, s_x, g * 16 + 16)
                stats(g, lambda t: x_all[:, bass.ds(g * TG + t, 1), :])
                dve.tensor_scalar(var[:, :], mv[:, :, 1], 1.0 + LN_EPS, LN_EPS ** 2, ALU.mult, ALU.add).then_inc(s_var, 1)
                wait(dve, s_sd, g + 1)
                link(dve.reciprocal(rs[:, :], sd[:, :]))
                follow()
                wait(dve, s_T, g)
                for t in range(TG):
                    dve.tensor_scalar(xhat[:, t, :], x_all[:, bass.ds(g * TG + t, 1), :].rearrange("p o d -> p (o d)"),
                                      mv[:, t, 0:1], rs[:, t:t + 1], ALU.subtract, ALU.mult).then_inc(s_xh, 1)

            def front_split(g):
                wait(dve, s_y, KH * g + KH)
                wait(dve, s_P, g * TG)
                link(dve.tensor_copy(y_h[:, :, :], y_f[:, :, :]))
                follow()
                dve.tensor_tensor(y_l[:, :, :], y_f[:, :, :], y_h[:, :, :].bitcast(f32), ALU.subtract).then_inc(s_ys, 1)

            def tile_a(g, gi, t):
                n = g * TG + t
                wait(dve, s_sq, n + 1)
                dve.tensor_reduce(ss[:, :], sq[:, :].rearrange("p (h d) -> p h d", d=DH), AX.X, ALU.add).then_inc(s_ss, 1)
                wait(dve, s_vh, n + 1)
                vs = lambda low: v_mm[:, bass.ds(gi * (TG * H) + t * H, H), (DH + 1) * low:(DH + 1) * low + DH]
                dve.scalar_tensor_tensor(out=vs(1), in0=ps_V[t % 2].rearrange("p (h d) -> p h d", h=H), scalar=CV,
                                         in1=vs(0), op0=ALU.mult, op1=ALU.subtract).then_inc(s_vl, 1)
                wait(dve, s_nr, n + 1)
                link(dve.scalar_tensor_tensor(out=nm[:, :], in0=nr[:, :], scalar=RMS_EPS, in1=rcol[:, :],
                                              op0=ALU.max, op1=ALU.mult))
                follow()
                link(dve.reciprocal(rn[:, :], nm[:, :]))
                follow()
                wait(dve, s_lo, n)
                wait(dve, s_hi, 2 * n)
                wait(dve, s_q2, n)
                dve.tensor_tensor(qk_n[:, :].rearrange("p (h d) -> p h d", d=DH),
                                  ps_QK[t % 2].rearrange("p (h d) -> p h d", d=DH),
                                  spread(rn[:, :], 2, DH), ALU.mult).then_inc(s_qkn, 1)
                wait(dve, s_hi, 2 * n + 2)
                dve.tensor_tensor(qk_s[:, :, DH:2 * DH], qk_n[:, :].rearrange("p (h d) -> p h d", d=DH),
                                  qk_s[:, :, 0:DH], ALU.subtract).then_inc(s_lo, 1)
                wait(dve, s_q2, n + 1)
                dve.tensor_reduce(qn2[:, bass.ds(gi * TG + t, 1), :].rearrange("p o h -> p (o h)"),
                                  q_sq[:, :].rearrange("p (h d) -> p h d", d=DH), AX.X, ALU.add).then_inc(s_qs, 1)
                wait(dve, s_T2, n + 1)
                dve.tensor_copy(q_T[:, :].rearrange("p (h n) -> p h n", h=H)[:, :, bass.ds(gi * (TG * P) + t * P, P)],
                                ps_TQ.rearrange("p (h n) -> p h n", h=H)).then_inc(s_qe, 1)

            a_body = TG * 2 + 1 + 1 + TG * 2
            with dve.Fori(0, NB) as b:
                with dve.Fori(0, NG) as gi:
                    g = b * NG + gi
                    chain[0], chain[1] = 0, g * a_body
                    front_ln(g)
                    front_split(g)
                    for t in range(TG):
                        tile_a(g, gi, t)
                    assert chain[0] == a_body, chain
                wait(dve, s_qs, b * NT + NT)
                dve.tensor_reduce(qmx[:, :], qn2[:, :, :].rearrange("p t h -> p h t"), AX.X, ALU.max).then_inc(s_mxD, 1)
                wait(dve, s_mxT, b + 1)
                dve.tensor_reduce(qmT[:, :], bank(0)[0:H, 0:P], AX.X, ALU.max).then_inc(s_mxD, 1)
                wait(dve, s_mxD, 3 * b + 2)
                dve.tensor_scalar(qmD[:, :], ident[0:H, 0:H], qmT[:, 0:1], None, ALU.mult).then_inc(s_mxD, 1)
                wait(dve, s_mx, b + 1)
                dve.tensor_scalar(nbias[:, :], nm[:, 0:H], CESC, None, ALU.mult).then_inc(s_nb, 1)
                wait(dve, s_nb, 2 * b + 1)
                dve.tensor_scalar(nbias[:, :], nbias[:, :], -KSCALE * math.sqrt(DH), TOP, ALU.mult, ALU.add).then_inc(s_nb, 1)

                def parts(hh, h, k):
                    s = hh * STEPS + k
                    if not (isinstance(h, int) and k < NEP):
                        wait(dve, s_PV, s - NEP + 1)
                    if k in ACT_H:
                        wait(dve, s_EhA, hh * len(ACT_H) + k // 2 + 1)
                    else:
                        wait(dve, s_E, s + 1)
                        dve.tensor_copy(e_h[:, k % NEP, :], e_f[:, k % NEF, :]).then_inc(s_EhD, 1)
                        wait(dve, s_EhD, hh * (STEPS - len(ACT_H)) + k // 2 + 1)
                    dve.tensor_tensor(e_l[:, k % NEP, :], e_f[:, k % NEF, :], e_h[:, k % NEP, :], ALU.subtract).then_inc(s_El, 1)

                def sum_out(unit, local):
                    wait(dve, s_OL, unit + 1)
                    a = attn[:, bass.ds(local * QT, QT), :] if not isinstance(local, int) else attn[:, local * QT:local * QT + QT, :]
                    lv = lsum[:, bass.ds(local * QT, QT)] if not isinstance(local, int) else lsum[:, local * QT:local * QT + QT]
                    dve.tensor_tensor(a.rearrange("p (b q) d -> p b q d", q=2), ps_O[:, :, :, 0:DH],
                                      ov_l[:, :, :].rearrange("p (b q) d -> p b q d", q=2), ALU.add).then_inc(s_Oev, 1)
                    dve.tensor_copy(lv.rearrange("p (b q) -> p b q", q=2), ps_O[:, :, :, DH]).then_inc(s_Oev, 1)

                def head_dve(b, h):
                    hh = b * H + h
                    for k in range(STEPS):
                        if k % NT == LAG - 1 and not (isinstance(h, int) and k < NT):
                            u = k // NT - 1
                            sum_out(hh * NQB + u, h * NQB + u)
                        parts(hh, h, k)

                head_dve(b, 0)
                with dve.Fori(1, H) as h:
                    head_dve(b, h)
                sum_out(b * H * NQB + H * NQB - 1, H * NQB - 1)

                c_body = 4 + 2 * (2 * TG + 1) + TG + 1 + 6 + 5 * TG
                with dve.Fori(0, NG) as gi:
                    g = b * NG + gi
                    cn = [0]

                    def clink(ins):
                        ins.then_inc(s_c, 1)
                        cn[0] += 1

                    def cfollow():
                        wait(dve, s_c, g * c_body + cn[0])

                    wait(dve, s_Oev, 2 * (b * H * NQB + H * NQB))
                    clink(dve.reciprocal(rl[:, :, :], lsum[:, :].rearrange("p (h t) -> p h t", h=H)[:, :, bass.ds(gi * TG, TG)]))
                    cfollow()
                    clink(dve.tensor_scalar(rl[:, :, :], rl[:, :, :], CIV, None, ALU.mult))
                    cfollow()
                    dve.tensor_tensor(xhat[:, :, :].rearrange("p t (h d) -> p h t d", h=H),
                                      attn[:, :, :].rearrange("p (h t) d -> p h t d", h=H)[:, :, bass.ds(gi * TG, TG), :],
                                      spread(rl[:, :, :], 3, DH), ALU.mult).then_inc(s_at, 1)
                    wait(dve, s_ah, g + 1)
                    dve.tensor_tensor(y_l[:, :, :], ps_T, y_h[:, :, :].bitcast(f32), ALU.subtract).then_inc(s_al, 1)
                    y = y_f[:, :, :].rearrange("p k (t d) -> p (k t) d", d=D)
                    for i in range(2):
                        wait(dve, s_Y, 2 * g + i + 1)
                        clink(dve.tensor_tensor(y[:, 2 * i:2 * i + 2, :], ps_Y[i].rearrange("p (t d) -> p t d", d=D),
                                                spread(bo_row[:, :], 1, 2), ALU.add))
                    cfollow()

                    def cstats(src):
                        for t in range(TG):
                            clink(dve.bn_stats(st[:, t, :], src(t)))
                        cfollow()
                        dve.sem_inc(s_held, 1)
                        for t in range(TG):
                            clink(dve.bn_aggr(mv[:, t, :], st[:, t, :]))
                        cfollow()

                    xs = lambda t: x_all[:, bass.ds(g * TG + t, 1), :].rearrange("p o d -> p (o d)")
                    cstats(lambda t: y[:, t, :])
                    dve.tensor_scalar(var[:, :], mv[:, :, 1], LN_EPS, None, ALU.add).then_inc(s_var3, 1)
                    wait(dve, s_sd3, 2 * g + 1)
                    clink(dve.reciprocal(rs[:, :], sd[:, :]))
                    cfollow()
                    for t in range(TG):
                        clink(dve.tensor_scalar(y[:, t, :], y[:, t, :], mv[:, t, 0:1], rs[:, t:t + 1], ALU.subtract, ALU.mult))
                    cfollow()
                    xg = x_all[:, bass.ds(g * TG, TG), :]
                    clink(dve.tensor_tensor(xg, xg, y, ALU.add))
                    cfollow()
                    cstats(xs)
                    dve.tensor_scalar(var[:, :], mv[:, :, 1], LN_EPS, None, ALU.add).then_inc(s_var3, 1)
                    wait(dve, s_sd3, 2 * g + 2)
                    clink(dve.reciprocal(rs[:, :], sd[:, :]))
                    cfollow()
                    for t in range(TG):
                        dve.tensor_scalar(xhat[:, t, :], xs(t), mv[:, t, 0:1], rs[:, t:t + 1], ALU.subtract, ALU.mult).then_inc(s_xn, 1)
                    wait(dve, s_nh, g + 1)
                    dve.tensor_tensor(y_l[:, :, :], ps_T, y_h[:, :, :].bitcast(f32), ALU.subtract).then_inc(s_nl, 1)
                    wait(dve, s_G, g + 1)
                    clink(dve.tensor_copy(gs[:, :, :], ps_G.rearrange("p (t e) -> p t e", e=NE)))
                    cfollow()
                    clink(dve.tensor_reduce(gm[:, :], gs[:, :, :], AX.X, ALU.max))
                    cfollow()
                    bc = lambda a: spread(a, 2, NE)
                    rk = spread(rank[:, :], 1, TG)
                    clink(dve.tensor_tensor(hot[:, :, :], gs[:, :, :], bc(gm[:, :]), ALU.is_equal))
                    cfollow()
                    clink(dve.tensor_tensor(hot[:, :, :], hot[:, :, :], rk, ALU.mult))
                    cfollow()
                    clink(dve.tensor_reduce(gm[:, :], hot[:, :, :], AX.X, ALU.max))
                    cfollow()
                    clink(dve.tensor_tensor(hot[:, :, :], rk, bc(gm[:, :]), ALU.is_equal))
                    cfollow()
                    for t in range(TG):
                        m = (g * TG + t) * NE
                        for e in range(NE):
                            if e % 2 == 0:
                                wait(dve, s_X, (g * TG + t) * XR + e // 2 + 1)
                            if e >= 2:
                                wait(dve, s_Xr, m + e - 1)
                            a = (f_a, f_b)[e % 2]
                            src, w = ps_X[e // 2][:, (e % 2) * D:(e % 2) * D + D], hot[:, t, e:e + 1]
                            if e == 1:
                                wait(dve, s_fin, g * TG + t)
                                dve.tensor_scalar(a[:, :], src, w, None, ALU.mult).then_inc(s_Xr, 1)
                            else:
                                dve.scalar_tensor_tensor(out=a[:, :], in0=src, scalar=w, in1=xhat[:, t, :] if e == 0 else a[:, :],
                                                         op0=ALU.mult, op1=ALU.add).then_inc(s_Xr, 1)
                        wait(dve, s_Xr, m + NE)
                        clink(dve.tensor_tensor(f_a[:, :], f_a[:, :], f_b[:, :], ALU.add))
                        cfollow()
                        clink(dve.bn_stats(st2[:, :], f_a[:, :]))
                        cfollow()
                        dve.sem_inc(s_held, 1)
                        clink(dve.bn_aggr(mv2[:, :], st2[:, :]))
                        cfollow()
                        dve.tensor_scalar(sc2[:, 0:1], mv2[:, 1:2], LN_EPS, None, ALU.add).then_inc(s_var5, 1)
                        wait(dve, s_sd5, g * TG + t + 1)
                        clink(dve.reciprocal(sc2[:, 2:3], sc2[:, 1:2]))
                        cfollow()
                        clink(dve.tensor_scalar(f_b[:, :], f_a[:, :], mv2[:, 0:1], sc2[:, 2:3], ALU.subtract, ALU.mult))
                        cfollow()
                        dve.tensor_tensor(xs(t), xs(t), f_b[:, :], ALU.add).then_inc(s_fin, 1)
                    assert cn[0] == c_body, (cn[0], c_body)

        @block.tensor
        def _(pe):
            start_at_one(pe, "pe")
            def split_mm(dst, terms, start=True):
                n = len(terms)
                for i, (l, r) in enumerate(terms):
                    ins = pe.matmul(dst, l, r, start=(i == 0), stop=(i == n - 1))
                return ins

            wait(pe, s_ones, 1)
            wait(pe, s_prepA, 1)
            pe.matmul(bank(0)[:, 0:1], ones[:, :], part[:, 0:1], start=True, stop=True).then_inc(s_prepP, 1)
            wait(pe, s_id, 4)
            wait(pe, s_prep, 3)
            wait(pe, s_ws, 1)

            def transpose_group(g, done):
                for k in range(KH):
                    for t in range(TG):
                        ins = pe.transpose(ps_T[:, k, t * P:(t + 1) * P], xhat[:, t, k * P:(k + 1) * P], ident[:, :])
                ins.then_inc(done, 1)

            def three(t, w_h, w_l, c0, c1):
                tok = slice(t * P, (t + 1) * P)
                return ([(y_h[:, k, tok], w_h[:, k, c0:c1]) for k in range(KH)]
                        + [(y_l[:, k, tok], w_h[:, k, c0:c1]) for k in range(KH)]
                        + [(y_h[:, k, tok], w_l[:, k, c0:c1]) for k in range(KH)])

            def project(g, t):
                n = g * TG + t
                wait(pe, s_qkn, n - 1 if t else n)
                wait(pe, s_vl, n - 1 if t else n)
                split_mm(ps_QK[t % 2], three(t, wqkv_h, wqkv_l, 0, 2 * D))
                split_mm(ps_V[t % 2], three(t, wqkv_h, wqkv_l, 2 * D, 3 * D)).then_inc(s_P, 1)

            def transpose_qk(g, t):
                n = g * TG + t
                wait(pe, s_lo, n + 1)
                wait(pe, s_qe, n)
                wait(pe, s_ke, n)
                for h in range(H):
                    pe.transpose(ps_TQ[:, h * P:(h + 1) * P], qk_s[:, h, 0:2 * DH], ident16[:, :])
                for h in range(H):
                    for a in range(2):
                        ins = pe.transpose(ps_TK[:, (2 * h + a) * P:(2 * h + a + 1) * P],
                                           qk_s[:, H + h, a * DH:(a + 2) * DH], ident16[:, :])
                ins.then_inc(s_T2, 1)

            with pe.Fori(0, NB) as b:
                with pe.Fori(0, NG) as gi:
                    g = b * NG + gi
                    wait(pe, s_xh, g * TG + TG)
                    wait(pe, s_y, KH * g)
                    transpose_group(g, s_T)
                    wait(pe, s_ys, g + 1)
                    for t in range(TG):
                        project(g, t)
                        if t:
                            transpose_qk(g, t - 1)
                    transpose_qk(g, TG - 1)
                wait(pe, s_mxD, 3 * b + 1)
                pe.transpose(bank(0)[0:H, 0:P], qmx[:, :], ident[:, :]).then_inc(s_mxT, 1)
                wait(pe, s_mxD, 3 * b + 3)
                pe.matmul(bank(0)[:, 0:H], ones[0:H, :], qmD[:, :], start=True, stop=True).then_inc(s_mxB, 1)
                wait(pe, s_mx, b + 1)
                wait(pe, s_ke, b * NT + NT)
                wait(pe, s_qe, b * NT + NT)

                def scores(hh, h, k):
                    s = hh * STEPS + k
                    qb, j = k // NT, k % NT
                    first = isinstance(h, int)
                    if not (first and k < 2):
                        wait(pe, s_E, s - 1)
                        if (k - 2) % 2 == 0:
                            wait(pe, s_EhA, (hh * STEPS + k) // 2 if False else hh * len(ACT_H) + k // 2)
                    nc.disable_value_cache = False
                    for a in range(2):
                        if first:
                            kt = k_T[:, a, h * N + j * P:h * N + (j + 1) * P]
                        else:
                            kt = k_T[:, a, bass.ds(h * N + j * P, P)]
                        for c in range(QB // BANK):
                            at = qb * QB + c * BANK
                            qt = q_T[:, h * N + at:h * N + at + BANK] if first else q_T[:, bass.ds(h * N + at, BANK)]
                            ins = pe.matmul(ps_S[k % 2][:, c * BANK:(c + 1) * BANK], kt, qt, start=(a == 0), stop=(a == 1),
                                            skip_group_check=True)
                    nc.disable_value_cache = True
                    ins.then_inc(s_S, 1)

                def pv(hh, h, k, unit):
                    s = hh * STEPS + k
                    j = k % NT
                    wait(pe, s_El, s + 1)
                    if j == 0:
                        wait(pe, s_Oev, 2 * unit)
                    at = j * H + h
                    v = (lambda w: v_mm[:, at, 0:w]) if isinstance(at, int) else (
                        lambda w: v_mm[:, bass.ds(at, 1), 0:w].rearrange("p o w -> p (o w)"))
                    nc.disable_value_cache = False
                    for q in range(QT):
                        for e, w in ((e_h, VW), (e_l, DH + 1)):
                            ins = pe.matmul(ps_O[:, q // 2, q % 2, 0:w], e[:, k % NEP, q * P:(q + 1) * P], v(w),
                                            start=(j == 0 and q % 2 == 0 and w == VW), stop=(j == NT - 1 and w != VW),
                                            skip_group_check=True)
                    nc.disable_value_cache = True
                    ins.then_inc(s_PV, 1)

                def head_pe(b, h):
                    hh = b * H + h
                    for k in range(STEPS):
                        scores(hh, h, k)
                        if k >= LAG:
                            pv(hh, h, k - LAG, hh * NQB + (k - LAG) // NT)
                        elif not isinstance(h, int):
                            pv(hh - 1, h - 1, STEPS + k - LAG, hh * NQB - 1)

                head_pe(b, 0)
                with pe.Fori(1, H) as h:
                    head_pe(b, h)
                for k in range(STEPS - LAG, STEPS):
                    pv(b * H + H - 1, H - 1, k, b * H * NQB + H * NQB - 1)

                wait(pe, s_ws, 4)
                with pe.Fori(0, NG) as gi:
                    g = b * NG + gi
                    wait(pe, s_at, g + 1)
                    wait(pe, s_E, (b * H + H) * STEPS)
                    wait(pe, s_Oev, 2 * (b * H * NQB + H * NQB))
                    transpose_group(g, s_T3)
                    wait(pe, s_al, g + 1)
                    for i in range(2):
                        for t in range(2 * i, 2 * i + 2):
                            ins = split_mm(ps_Y[i][:, (t % 2) * D:(t % 2 + 1) * D], three(t, wo_h, wo_l, 0, D))
                        ins.then_inc(s_Y, 1)
                    wait(pe, s_xn, g * TG + TG)
                    transpose_group(g, s_T4)
                    wait(pe, s_nl, g + 1)
                    for t in range(TG):
                        ins = split_mm(ps_G[:, t * NE:(t + 1) * NE], three(t, wg_h, wg_l, 0, NE))
                    ins.then_inc(s_G, 1)
                    for t in range(TG):
                        for c in range(XR):
                            if t:
                                wait(pe, s_Xr, (g * TG + t - 1) * NE + 2 * c + 2)
                            split_mm(ps_X[c], three(t, we_h, we_l, c * BANK, (c + 1) * BANK)).then_inc(s_X, 1)


def kernel(**inputs):
    import numpy as np
    import concourse.bacc as bacc
    from concourse.bass_utils import run_bass_kernel_spmd

    def get(name):
        return np.asarray(inputs[name])

    we = get("L0_ffn_expert_w")
    arrays = {
        "x": get("L0_attn_x"),
        "wqkvT": np.concatenate([get("L0_attn_w_" + n).T for n in "qkv"], axis=1),
        "woT": get("L0_attn_w_o").T,
        "weT": we.transpose(2, 0, 1).reshape(we.shape[2], -1),
        "wgT": get("L0_ffn_gate_w").T,
        "ln_gamma": get("L0_attn_ln_gamma"),
        "ln_beta": get("L0_attn_ln_beta"),
        "q_gamma": get("L0_attn_q_gamma"),
        "k_gamma": get("L0_attn_k_gamma"),
        "b_o": get("L0_attn_b_o"),
    }
    arrays = {n: np.ascontiguousarray(a) for n, a in arrays.items()}
    nc = bacc.Bacc("TRN2", target_bir_lowering=False, num_devices=1)
    args = [nc.dram_tensor(n, a.shape, mybir.dt.from_np(a.dtype), kind="ExternalInput").ap() for n, a in arrays.items()]
    x = arrays["x"]
    out = nc.dram_tensor("out", x.shape, mybir.dt.from_np(x.dtype), kind="ExternalOutput").ap()
    build(nc, *args, out)
    return run_bass_kernel_spmd(nc, [arrays], core_ids=[0]).results[0]["out"]
```

```python
import math
from contextlib import ExitStack

import concourse.bass as bass
from concourse import mybir


def build(nc, x, wqkvT, woT, weT, wgT, ln_gamma, ln_beta, q_gamma, k_gamma, b_o, out):
    f32, f32r, f16, u32 = mybir.dt.float32, mybir.dt.float32r, mybir.dt.float16, mybir.dt.uint32
    ALU, ACT, AX = mybir.AluOpType, mybir.ActivationFunctionType, mybir.AxisListType
    P = 128
    NB, N, D = x.shape
    DH = q_gamma.shape[0]
    H = D // DH
    KH = D // P
    NE = wgT.shape[1]
    NT = N // P
    TG = 4
    NG = NT // TG
    QB = 1024
    NQB = N // QB
    QT = QB // P
    BANK = 512
    STEPS = NQB * NT
    LAG = 4
    NEF, NEP = 4, 4
    VW = DH + 1 + DH
    VS = VW + 1
    XR = 4
    NX = NE
    LN_EPS, RMS_EPS = 1e-5, 1e-8
    KSCALE = 32.0
    QMAX = 512.0
    TOP = 10.5

    nc.disable_value_cache = True
    with ExitStack() as ctx:
        def sb(name, shape, dt):
            return ctx.enter_context(nc.sbuf_tensor(name, shape, dt))

        def sem(name):
            return ctx.enter_context(nc.semaphore(name))

        x_all = sb("x_all", [P, NT, D], f32)
        wqkv_h, wqkv_l = (sb(n, [P, KH, 3 * D], f32r) for n in ("wqkv_h", "wqkv_l"))
        wo_h, wo_l = (sb(n, [P, KH, D], f32r) for n in ("wo_h", "wo_l"))
        we_h, we_l = (sb(n, [P, KH, NE * D], f32r) for n in ("we_h", "we_l"))
        wg_h, wg_l = (sb(n, [P, KH, NE], f32r) for n in ("wg_h", "wg_l"))
        q_T = sb("q_T", [P, H * N], f16)
        k_T = sb("k_T", [P, 2, H * N], f16)
        v_mm = sb("v_mm", [P, NT * H, VS], f16)
        attn = sb("attn", [P, H * NQB * QT, DH], f32)
        lsum = sb("lsum", [P, H * NQB * QT], f32)
        e_f = sb("e_f", [P, NEF, QB], f32)
        e_h, e_l = (sb(n, [P, NEP, QB], f16) for n in ("e_h", "e_l"))
        ov_l = sb("ov_l", [P, QT, DH], f32)
        y_h, y_l = (sb(n, [P, KH, TG * P], f32r) for n in ("y_h", "y_l"))
        n_h, n_l = (sb(n, [P, KH, TG * P], f32r) for n in ("n_h", "n_l"))
        e_f32 = e_f[:, :, :].rearrange("p s n -> p (s n)")
        y_f = e_f32[:, 0:KH * TG * P].rearrange("p (k n) -> p k n", k=KH)
        sq = [e_f32[:, (2 + i) * 2 * D:(3 + i) * 2 * D] for i in range(2)]
        e_l16 = e_l[:, :, :].rearrange("p s n -> p (s n)")
        qk_n = [e_l16[:, i * 4 * D:(i + 1) * 4 * D].bitcast(f32) for i in range(2)]
        e_h16 = e_h[:, :, :].rearrange("p s n -> p (s n)")
        xhat = e_h16[:, 0:2 * TG * D].bitcast(f32).rearrange("p (t d) -> p t d", d=D)
        qk_s = [a[:, 2048:2048 + 6 * H * DH].rearrange("p (h c) -> p h c", h=2 * H)
                for a in (e_h16, e_l16)]
        q_sq = e_h16[:, 3584:3584 + 2 * D].bitcast(f32)
        k32 = k_T[:, :, :].rearrange("p a n -> p (a n)").bitcast(f32)
        q32 = q_T[:, :].bitcast(f32)
        xa = q32[:, 0:TG * D].rearrange("p (t d) -> p t d", d=D)
        xn = q32[:, TG * D:2 * TG * D].rearrange("p (t d) -> p t d", d=D)
        xe = k32[:, 0:NT * D].rearrange("p (t d) -> p t d", d=D)
        f_b = k32[:, NT * D:(NT + 2) * D].rearrange("p (i d) -> p i d", d=D)
        ident = sb("ident", [P, P], f32)
        ident16 = sb("ident16", [P, P], f16)
        ones = sb("ones", [P, P], f32)
        gam, bet = (sb(n, [P, KH], f32) for n in ("gam", "bet"))
        gam_row, bet_row = (e_f32[:, i * D:(i + 1) * D] for i in range(2))
        bo_row = sb("bo_row", [P, D], f32)
        qg_row, kg_row = (sb(n, [P, DH], f32) for n in ("qg_row", "kg_row"))
        gq = sb("gq", [P, DH], f32)
        c_ = sb("c_", [P, 24], f32)
        part = sb("part", [P, 4], f32)
        st = sb("st", [P, TG, 6], f32)
        mv = sb("mv", [P, TG, 2], f32)
        var, sd, rs = (sb(n, [P, TG], f32) for n in ("var", "sd", "rs"))
        ss, nr, nm, rn = (sb(n, [P, 2 * H], f32) for n in ("ss", "nr", "nm", "rn"))
        rcol = sb("rcol", [P, 2 * H], f32)
        qn2 = sb("qn2", [P, NT, H], f32)
        qmx = sb("qmx", [P, H], f32)
        qmT = sb("qmT", [H, 1], f32)
        qmD = sb("qmD", [H, H], f32)
        nbias = sb("nbias", [P, H], f32)
        rl = sb("rl", [P, H, NT], f32)
        gs = sb("gs", [P, TG, NE], f32)
        gm = sb("gm", [P, TG], f32)
        hot = sb("hot", [P, TG, NE], f32)
        rank = sb("rank", [P, NE], f32)
        st5 = sb("st5", [P, TG, 6], f32)
        mv5 = sb("mv5", [P, TG, 2], f32)
        var5, sd5, rs5 = (sb(n, [P, TG], f32) for n in ("var5", "sd5", "rs5"))

        banks = ctx.enter_context(nc.psum_tensor("banks", [P, 8 * BANK], f32))

        def bank(i, n=1):
            return banks[:, i * BANK:(i + n) * BANK]

        ps_S = [bank(0, 2), bank(2, 2)]
        ps_O = bank(4, 4).rearrange("p (b c) -> p b c", c=BANK)[:, :, 0:2 * VW].rearrange(
            "p b (q c) -> p b q c", c=VW)
        ps_T = bank(0, 2).rearrange("p (k c) -> p k c", k=KH)
        ps_QK = [bank(2), bank(3)]
        ps_V = [bank(4)[:, 0:D], bank(5)[:, 0:D]]
        ps_TQ = bank(6).bitcast(f16)[:, 0:H * P]
        ps_TK = bank(7).bitcast(f16)[:, 0:2 * H * P]
        ps_X = [bank(2 + i) for i in range(XR)]
        ps_Y = [bank(6), bank(7)]
        ps_T3 = bank(6, 2).rearrange("p (k c) -> p k c", k=KH)
        ps_G = bank(0)[:, 0:TG * NE]

        raw_we = k_T[:, :, :].rearrange("p a n -> p (a n)").bitcast(f32)[:, 0:KH * NE * D].rearrange(
            "p (k n) -> p k n", k=KH)
        raw_q = q_T[:, :].bitcast(f32)
        raw_wqkv = raw_q[:, 0:KH * 3 * D].rearrange("p (k n) -> p k n", k=KH)
        raw_wo = raw_q[:, KH * 3 * D:KH * 4 * D].rearrange("p (k n) -> p k n", k=KH)
        raw_wg = sb("raw_wg", [P, KH, NE], f32)

        CQ, CESC, CV, CIV = (c_[:, i:i + 1] for i in range(4))
        tmp = [c_[:, i:i + 1] for i in range(4, 16)]

        owned = {}

        def sems(owner, names, first=2):
            made = [sem("s_" + n) for n in names.split()]
            owned.setdefault(owner, []).extend((m, first) for m in made)
            return made

        def start_of(s):
            return next((first for group in owned.values() for m, first in group if m is s), 0)

        def wait(eng, s, value):
            eng.wait_ge(s, value + start_of(s))

        def start_up(eng, owner):
            for s, first in owned.get(owner, []):
                eng.sem_inc(s, first)

        s_x, s_small, s_wq, s_we, s_out = (sem("s_" + n) for n in "x small wq we out".split())
        s_id, s_rank, s_ones, s_qg, s_q2 = sems("pool", "id rank ones qg q2")
        s_at, s_xa, s_fs, s_fin = sems("pool", "at xa fs fin")
        s_prep, s_const, s_ws = sems("dve", "prep const ws")
        s_dve, s_dq, s_var, s_xh, s_ys, s_ss, s_qkn, s_lo, s_vl, s_qe, s_qs, s_mxD, s_nb = sems(
            "dve", "dve dq var xh ys ss qkn lo vl qe qs mxD nb")
        s_held, = sems("dve", "held")
        s_EhD, s_El, s_Oev = sems("dve", "EhD El Oev")
        s_c, s_rl, s_al, s_yb, s_var3, s_yn, s_xn, s_nl, s_Gr, s_c5, s_var5, s_f5 = sems(
            "dve", "c rl al yb var3 yn xn nl Gr c5 var5 f5")
        s_Xr, = sems("dve", "Xr", NX + 1)
        s_prepA, s_wh, s_sd, s_y, s_yh, s_sq, s_vh, s_nr, s_hi, s_ke, s_mx = sems("act", "prepA wh sd y yh sq vh nr hi ke mx")
        s_E, s_EhA, s_OL, s_ah, s_sd3, s_nh, s_sd5, s_xc = sems("act", "E EhA OL ah sd3 nh sd5 xc")
        s_prepP, s_T, s_P, s_T2, s_mxT, s_mxB = sems("pe", "prepP T P T2 mxT mxB")
        s_S, s_PV, s_T3, s_Y, s_T4, s_G, s_X = sems("pe", "S PV T3 Y T4 G X")

        x_d = x.rearrange("b (t p) d -> p (b t) d", p=P)
        out_d = out.rearrange("b (t p) d -> p (b t) d", p=P)

        def spread(ap, axis, n):
            ap = ap.unsqueeze(axis)
            shape = list(ap.shape)
            shape[axis] = n
            return ap.to_broadcast(shape)

        def groups(eng, body):
            body(0, first=True)
            with eng.Fori(1, NG - 1) as gi:
                body(gi)
            body(NG - 1, last=True)

        class Chain:
            def __init__(self, eng, s, per):
                self.eng, self.s, self.per = eng, s, per

            def begin(self, g, n=0):
                self.g, self.n = g, n

            def link(self, ins):
                ins.then_inc(self.s, 1)
                self.n += 1
                assert self.n <= self.per

            def follow(self):
                wait(self.eng, self.s, self.g * self.per + self.n)

        ACT_H = [k for k in range(STEPS) if k % 2 == 0]

        def act_h(k):
            return sum(j < k for j in ACT_H)

        block = ctx.enter_context(nc.Block())

        @block.sync
        def _(sp):
            sp.dma_start(x_all[:, 0:TG, :], x_d[:, 0:TG, :]).then_inc(s_x, 16)
            sp.dma_start(raw_wqkv, wqkvT.rearrange("(k p) n -> p k n", p=P)).then_inc(s_wq, 16)
            sp.dma_start(raw_wo, woT.rearrange("(k p) n -> p k n", p=P)).then_inc(s_wq, 16)
            with sp.Fori(1, NG) as gi:
                wait(sp, s_x, gi * 16)
                sp.dma_start(x_all[:, bass.ds(gi * TG, TG), :], x_d[:, bass.ds(gi * TG, TG), :]).then_inc(s_x, 16)

            def store(b, gi):
                g = b * NG + gi
                wait(sp, s_fin, g + 1)
                sp.dma_start(out_d[:, bass.ds(g * TG, TG), :], x_all[:, bass.ds(gi * TG, TG), :]).then_inc(s_out, 16)

            with sp.Fori(0, NB - 1) as b:
                with sp.Fori(0, NG) as gi:
                    store(b, gi)
                    g = b * NG + gi
                    wait(sp, s_out, (g + 1) * 16)
                    wait(sp, s_x, (g + NG) * 16)
                    sp.dma_start(x_all[:, bass.ds(gi * TG, TG), :], x_d[:, bass.ds((g + NG) * TG, TG), :]).then_inc(s_x, 16)
            with sp.Fori(0, NG) as gi:
                store(NB - 1, gi)
            wait(sp, s_out, NB * NG * 16)

        @block.gpsimd
        def _(pool):
            start_up(pool, "pool")
            for m in (ident, ident16):
                pool.memset(m[:, :], 0.0).then_inc(s_id, 1)
            pool.memset(ones[:, :], 1.0).then_inc(s_ones, 1)
            for e in range(NE):
                pool.memset(rank[:, e:e + 1], float(NE - e)).then_inc(s_rank, 1)
            for i in range(2 * H):
                pool.memset(rcol[:, i:i + 1], 1.0 if i < H else 1.0 / KSCALE).then_inc(s_rank, 1)
            pool.memset(v_mm[:, :, DH:DH + 1], 1.0).then_inc(s_ones, 1)
            wait(pool, s_id, 2)
            for m in (ident, ident16):
                pool.affine_select(out=m[:, :], in_=m[:, :], compare_op=ALU.not_equal, fill=1.0, base=0,
                                   pattern=[[-1, P]], channel_multiplier=1).then_inc(s_id, 1)
            wait(pool, s_const, 1)
            with pool.Fori(0, NB) as b:
                with pool.Fori(0, NG) as gi:
                    for t in range(TG):
                        n = (b * NG + gi) * TG + t
                        qn = qk_n[t % 2][:, 0:D]
                        qv = qn.rearrange("p (h d) -> p h d", h=H)
                        wait(pool, s_qkn, n + 1)
                        pool.tensor_tensor(qv, qv, spread(gq[:, :], 1, H), ALU.mult).then_inc(s_qg, 1)
                        wait(pool, s_qg, n + 1)
                        wait(pool, s_qs, n)
                        pool.tensor_tensor(q_sq[:, :], qn, qn, ALU.mult).then_inc(s_q2, 1)

                def normalise(gi):
                    tiles = bass.ds(gi * TG, TG)
                    wait(pool, s_T3, b * NG + gi)
                    pool.tensor_tensor(xa.rearrange("p t (h d) -> p h t d", h=H),
                                       attn[:, :, :].rearrange("p (h t) d -> p h t d", h=H)[:, :, tiles, :],
                                       spread(rl[:, :, tiles], 3, DH), ALU.mult).then_inc(s_at, 1)

                def residual(gi):
                    g = b * NG + gi
                    y = y_f[:, :, :].rearrange("p k (t d) -> p (k t) d", d=D)
                    wait(pool, s_yn, g * TG + TG)
                    xg = x_all[:, bass.ds(gi * TG, TG), :]
                    pool.tensor_tensor(xg, xg, y, ALU.add).then_inc(s_xa, 1)

                def expert_sum(gi, t):
                    n = (b * NG + gi) * TG + t
                    xt = xe[:, bass.ds(gi * TG + t, 1), :].rearrange("p o d -> p (o d)")
                    wait(pool, s_Xr, n * NE + NE)
                    pool.tensor_tensor(xt, xt, f_b[:, t % 2, :], ALU.add).then_inc(s_fs, 1)

                def finish(gi):
                    g = b * NG + gi
                    wait(pool, s_f5, g * TG + TG)
                    xg = x_all[:, bass.ds(gi * TG, TG), :]
                    pool.tensor_tensor(xg, xg, xe[:, bass.ds(gi * TG, TG), :], ALU.add).then_inc(s_fin, 1)

                def c_pool(gi, first=False, last=False, more=True):
                    for t in range(TG):
                        expert_sum(gi, t)
                        if t == 1 and not last:
                            residual(gi + 1)
                        if t == 1 and not first:
                            finish(gi - 1)
                        if t == 1 and more:
                            normalise(gi + 2)

                wait(pool, s_rl, 2 * b + 2)
                wait(pool, s_Oev, 2 * (b * H * NQB + H * NQB))
                wait(pool, s_S, (b * H + H) * STEPS)
                normalise(0)
                normalise(1)
                residual(0)
                c_pool(0, first=True)
                with pool.Fori(1, NG - 2) as gi:
                    c_pool(gi)
                c_pool(NG - 2, more=False)
                c_pool(NG - 1, last=True, more=False)
                finish(NG - 1)

        @block.scalar
        def _(act):
            start_up(act, "act")
            for col, src in ((gam, ln_gamma), (bet, ln_beta)):
                for k in range(KH):
                    act.dma_start(col[:, k:k + 1], src[k * P:(k + 1) * P].rearrange("(p o) -> p o", o=1)).then_inc(s_small, 16)
            for dst, src in ((gam_row, ln_gamma), (bet_row, ln_beta), (bo_row, b_o), (qg_row, q_gamma), (kg_row, k_gamma)):
                act.dma_start(dst[:, :], src.partition_broadcast(P)).then_inc(s_small, 16)
            act.dma_start(raw_wg[:, :, :], wgT.rearrange("(k p) n -> p k n", p=P)).then_inc(s_small, 16)
            act.dma_start(raw_we, weT.rearrange("(k p) n -> p k n", p=P)).then_inc(s_we, 16)
            wait(act, s_wq, 32)
            act.activation(wqkv_h[:, :, :], raw_wqkv, ACT.Copy).then_inc(s_wh, 1)
            act.activation(wo_h[:, :, :], raw_wo, ACT.Copy).then_inc(s_wh, 1)
            wait(act, s_small, 160)
            act.activation(wg_h[:, :, :], raw_wg[:, :, :], ACT.Copy).then_inc(s_wh, 1)
            act.activation(xhat[:, 0:KH, :], raw_wqkv[:, :, 2 * D:3 * D], ACT.Square, accum_out=part[:, 0:1]).then_inc(s_prepA, 1)
            act.activation(sq[0][:, 0:D], gam_row[:, :], ACT.Square, accum_out=part[:, 1:2]).then_inc(s_prepA, 1)
            act.activation(sq[0][:, D:2 * D], bet_row[:, :], ACT.Square, accum_out=part[:, 2:3]).then_inc(s_prepA, 1)
            wait(act, s_we, 16)
            act.activation(we_h[:, :, :], raw_we, ACT.Copy).then_inc(s_wh, 1)
            wait(act, s_prep, 6)
            act.activation(tmp[7], tmp[6], ACT.Sqrt).then_inc(s_prepA, 1)

            with act.Fori(0, NB) as b:
                def root(g):
                    wait(act, s_var, g + 1)
                    act.activation(sd[:, :], var[:, :], ACT.Sqrt).then_inc(s_sd, 1)

                def affine(g, dst, done):
                    for k in range(KH):
                        act.activation(dst[:, k, :], ps_T[:, k, :], ACT.Identity, bias=bet[:, k:k + 1],
                                       scale=gam[:, k:k + 1]).then_inc(done, 1)

                def whole_y(g):
                    wait(act, s_T, g + 1)
                    wait(act, s_ys, g)
                    affine(g, y_f, s_y)

                def high_y(g):
                    wait(act, s_P, g * TG)
                    affine(g, y_h, s_yh)

                def squares(n, at, t):
                    wait(act, s_P, n + 1)
                    wait(act, s_ss, n - 1)
                    act.activation(sq[t % 2], ps_QK[t % 2], ACT.Square).then_inc(s_sq, 1)
                    act.activation(v_mm[:, bass.ds(at * H, H), 0:DH], ps_V[t % 2].rearrange("p (h d) -> p h d", h=H),
                                   ACT.Copy, scale=CV).then_inc(s_vh, 1)

                def norms(n):
                    wait(act, s_ss, n + 1)
                    act.activation(nr[:, :], ss[:, :], ACT.Sqrt, scale=1.0 / DH).then_inc(s_nr, 1)

                def high_qk(n, t):
                    qn, qs = qk_n[t % 2], qk_s[t % 2]
                    wait(act, s_qg, n + 1)
                    wait(act, s_T2, n - 1)
                    act.activation(qs[:, :, 0:DH], qn.rearrange("p (h d) -> p h d", d=DH), ACT.Copy).then_inc(s_hi, 1)
                    act.activation(qs[:, H:, 2 * DH:], qn[:, D:].rearrange("p (h d) -> p h d", d=DH), ACT.Copy).then_inc(s_hi, 1)

                def move_k(n, at):
                    wait(act, s_T2, n + 1)
                    act.activation(k_T[:, :, :].rearrange("p a (h n) -> p h a n", h=H)[:, :, :, bass.ds(at * P, P)],
                                   ps_TK.rearrange("p (h a n) -> p h a n", h=H, a=2), ACT.Copy).then_inc(s_ke, 1)

                def a_act(gi, first=False, last=False):
                    g = b * NG + gi
                    for t in range(TG):
                        n, at = g * TG + t, gi * TG + t
                        squares(n, at, t)
                        norms(n)
                        if not (first and t < 1):
                            high_qk(n - 1, t - 1)
                        if t == 0 and not last:
                            root(g + 1)
                        if t == 2 and not last:
                            high_y(g + 1)
                        if not (first and t < 2):
                            move_k(n - 2, at - 2)
                        if t == 1 and not last:
                            whole_y(g + 1)

                root(b * NG)
                whole_y(b * NG)
                high_y(b * NG)
                groups(act, a_act)
                end = b * NT + NT
                high_qk(end - 1, NT - 1)
                move_k(end - 2, NT - 2)
                move_k(end - 1, NT - 1)
                wait(act, s_mxB, b + 1)
                act.activation(nm[:, 0:H], bank(0)[:, 0:H], ACT.Sqrt).then_inc(s_mx, 1)
                wait(act, s_nb, 2 * b + 2)

                def exp_step(hh, h, k):
                    s = hh * STEPS + k
                    wait(act, s_S, s + 1)
                    if not (isinstance(h, int) and k < NEF):
                        wait(act, s_El, s - NEF + 1)
                    act.activation(e_f[:, k % NEF, :], ps_S[k % 2], ACT.Exp, bias=bias_of(h), scale=CESC).then_inc(s_E, 1)
                    j = k - 1
                    if j in ACT_H:
                        if not (isinstance(h, int) and j < NEP):
                            wait(act, s_PV, s - NEP)
                        wait(act, s_E, s)
                        act.activation(e_h[:, j % NEP, :], e_f[:, j % NEF, :], ACT.Copy).then_inc(s_EhA, 1)

                def low_out(unit):
                    wait(act, s_PV, unit * NT + NT)
                    wait(act, s_Oev, 2 * unit)
                    act.activation(ov_l[:, :, :].rearrange("p (b q) d -> p b q d", q=2), ps_O[:, :, :, DH + 1:],
                                   ACT.Copy).then_inc(s_OL, 1)

                def bias_of(h):
                    return nbias[:, h:h + 1] if isinstance(h, int) else nbias[:, bass.ds(h, 1)]

                def head_act(b, h):
                    hh = b * H + h
                    for k in range(STEPS):
                        exp_step(hh, h, k)
                        if k % NT == LAG - 1 and not (isinstance(h, int) and k < NT):
                            low_out(hh * NQB + k // NT - 1)

                head_act(b, 0)
                with act.Fori(1, H) as h:
                    head_act(b, h)
                low_out(b * H * NQB + H * NQB - 1)

                def front_act(g):
                    wait(act, s_T3, g + 1)
                    wait(act, s_Y, 2 * g)
                    act.activation(y_h[:, :, :], ps_T3, ACT.Copy).then_inc(s_ah, 1)

                def root3(g, i):
                    wait(act, s_var3, 2 * g + i + 1)
                    act.activation(sd[:, :], var[:, :], ACT.Sqrt).then_inc(s_sd3, 1)

                def high_n(g, gi):
                    wait(act, s_xn, g * TG + TG)
                    act.activation(xe[:, bass.ds(gi * TG, TG), :], xn, ACT.Copy).then_inc(s_xc, 1)
                    wait(act, s_T4, g + 1)
                    wait(act, s_X, g * TG * XR)
                    act.activation(n_h[:, :, :], ps_T, ACT.Copy).then_inc(s_nh, 1)

                def root5(g):
                    wait(act, s_var5, g + 1)
                    act.activation(sd5[:, :], var5[:, :], ACT.Sqrt).then_inc(s_sd5, 1)

                def c_act(gi, first=False, last=False):
                    g = b * NG + gi
                    if not last:
                        front_act(g + 1)
                    if not first:
                        root5(g - 1)
                    if not last:
                        root3(g + 1, 0)
                        root3(g + 1, 1)
                        high_n(g + 1, gi + 1)

                front_act(b * NG)
                root3(b * NG, 0)
                root3(b * NG, 1)
                high_n(b * NG, 0)
                groups(act, c_act)
                root5(b * NG + NG - 1)

        @block.vector
        def _(dve):
            start_up(dve, "dve")
            wait(dve, s_prepP, 1)
            wait(dve, s_prepA, 3)
            dve.tensor_scalar(tmp[4], part[:, 1:2], float(D), None, ALU.mult).then_inc(s_prep, 1)
            wait(dve, s_prep, 1)
            dve.tensor_tensor(tmp[5], tmp[4], part[:, 2:3], ALU.add).then_inc(s_prep, 1)
            wait(dve, s_prep, 2)
            dve.tensor_scalar(tmp[8], bank(0)[:, 0:1], 2.0, None, ALU.mult).then_inc(s_prep, 1)
            wait(dve, s_prep, 3)
            dve.tensor_tensor(tmp[9], tmp[5], tmp[8], ALU.mult).then_inc(s_prep, 1)
            wait(dve, s_prep, 4)
            dve.tensor_scalar(tmp[10], tmp[9], 1e-30, None, ALU.max).then_inc(s_prep, 1)
            wait(dve, s_prep, 5)
            dve.tensor_scalar(tmp[6], tmp[10], 2.0 ** -28, None, ALU.mult).then_inc(s_prep, 1)
            wait(dve, s_small, 160)
            dve.tensor_tensor(gq[:, :], qg_row[:, :], kg_row[:, :], ALU.mult).then_inc(s_prep, 1)
            wait(dve, s_prep, 7)
            dve.tensor_reduce(tmp[0], gq[:, :], AX.X, ALU.max, apply_absolute_value=True).then_inc(s_prep, 1)
            wait(dve, s_prep, 8)
            dve.tensor_scalar(tmp[1], tmp[0], 1e-30, 1.0 / QMAX, ALU.max, ALU.mult).then_inc(s_prep, 1)
            wait(dve, s_prep, 9)
            dve.reciprocal(tmp[2], tmp[1]).then_inc(s_prep, 1)
            wait(dve, s_prepA, 4)
            dve.reciprocal(tmp[11], tmp[7]).then_inc(s_prep, 1)
            wait(dve, s_prep, 11)
            dve.tensor_scalar(CQ.bitcast(u32), tmp[2].bitcast(u32), 0x7F800000, None, ALU.bitwise_and).then_inc(s_prep, 1)
            dve.tensor_scalar(CV.bitcast(u32), tmp[11].bitcast(u32), 0x7F800000, None, ALU.bitwise_and).then_inc(s_prep, 1)
            wait(dve, s_prep, 13)
            dve.reciprocal(CIV, CV).then_inc(s_prep, 1)
            dve.reciprocal(tmp[3], CQ).then_inc(s_prep, 1)
            wait(dve, s_prep, 15)
            dve.tensor_scalar(CESC, tmp[3], 1.0 / (KSCALE * math.sqrt(DH)), None, ALU.mult).then_inc(s_prep, 1)
            wait(dve, s_prep, 16)
            dve.tensor_scalar(gq[:, :], gq[:, :], CQ, None, ALU.mult).then_inc(s_const, 1)
            for i, (w, hi, lo) in enumerate(((raw_wqkv, wqkv_h, wqkv_l), (raw_wo, wo_h, wo_l), (raw_wg[:, :, :], wg_h, wg_l), (raw_we, we_h, we_l))):
                wait(dve, s_wh, i + 1)
                dve.tensor_tensor(lo[:, :, :], w, hi[:, :, :].bitcast(f32), ALU.subtract).then_inc(s_ws, 1)

            ln_a = Chain(dve, s_dve, 2 * TG + 1)
            qk_a = Chain(dve, s_dq, 2)
            with dve.Fori(0, NB) as b:
                def group_stats(g, gi):
                    wait(dve, s_x, g * 16 + 16)
                    ln_a.begin(g)
                    for t in range(TG):
                        ln_a.link(dve.bn_stats(st[:, t, :], x_all[:, bass.ds(gi * TG + t, 1), :]))
                    ln_a.follow()
                    dve.sem_inc(s_held, 1)
                    for t in range(TG):
                        ln_a.link(dve.bn_aggr(mv[:, t, :], st[:, t, :]))
                    ln_a.follow()
                    dve.tensor_scalar(var[:, :], mv[:, :, 1], 1.0 + LN_EPS, LN_EPS ** 2, ALU.mult, ALU.add).then_inc(s_var, 1)

                def group_normal(g, gi):
                    wait(dve, s_sd, g + 1)
                    ln_a.link(dve.reciprocal(rs[:, :], sd[:, :]))
                    ln_a.follow()
                    wait(dve, s_T, g)
                    for t in range(TG):
                        dve.tensor_scalar(xhat[:, t, :], x_all[:, bass.ds(gi * TG + t, 1), :].rearrange("p o d -> p (o d)"),
                                          mv[:, t, 0:1], rs[:, t:t + 1], ALU.subtract, ALU.mult).then_inc(s_xh, 1)

                def low_y(g):
                    wait(dve, s_yh, KH * g + KH)
                    wait(dve, s_P, g * TG)
                    dve.tensor_tensor(y_l[:, :, :], y_f[:, :, :], y_h[:, :, :].bitcast(f32), ALU.subtract).then_inc(s_ys, 1)

                def sums(n, at, t):
                    wait(dve, s_sq, n + 1)
                    dve.tensor_reduce(ss[:, :], sq[t % 2].rearrange("p (h d) -> p h d", d=DH), AX.X, ALU.add).then_inc(s_ss, 1)
                    wait(dve, s_vh, n + 1)
                    v = v_mm[:, bass.ds(at * H, H), :]
                    dve.scalar_tensor_tensor(out=v[:, :, DH + 1:VW], in0=ps_V[t % 2].rearrange("p (h d) -> p h d", h=H),
                                             scalar=CV, in1=v[:, :, 0:DH], op0=ALU.mult, op1=ALU.subtract).then_inc(s_vl, 1)

                def normal_qk(n, t):
                    wait(dve, s_nr, n + 1)
                    qk_a.begin(n)
                    qk_a.link(dve.scalar_tensor_tensor(out=nm[:, :], in0=nr[:, :], scalar=RMS_EPS, in1=rcol[:, :],
                                                       op0=ALU.max, op1=ALU.mult))
                    qk_a.follow()
                    qk_a.link(dve.reciprocal(rn[:, :], nm[:, :]))
                    qk_a.follow()
                    wait(dve, s_lo, n - 1)
                    wait(dve, s_hi, 2 * n - 2)
                    wait(dve, s_q2, n - 1)
                    dve.tensor_tensor(qk_n[t % 2].rearrange("p (h d) -> p h d", d=DH),
                                      ps_QK[t % 2].rearrange("p (h d) -> p h d", d=DH),
                                      spread(rn[:, :], 2, DH), ALU.mult).then_inc(s_qkn, 1)

                def low_qk(n, at, t):
                    wait(dve, s_hi, 2 * n + 2)
                    qs = qk_s[t % 2]
                    dve.tensor_tensor(qs[:, :, DH:2 * DH], qk_n[t % 2].rearrange("p (h d) -> p h d", d=DH),
                                      qs[:, :, 0:DH], ALU.subtract).then_inc(s_lo, 1)
                    wait(dve, s_q2, n + 1)
                    dve.tensor_reduce(qn2[:, bass.ds(at, 1), :].rearrange("p o h -> p (o h)"),
                                      q_sq[:, :].rearrange("p (h d) -> p h d", d=DH), AX.X, ALU.add).then_inc(s_qs, 1)

                def move_q(n, at):
                    wait(dve, s_T2, n + 1)
                    dve.tensor_copy(q_T[:, :].rearrange("p (h n) -> p h n", h=H)[:, :, bass.ds(at * P, P)],
                                    ps_TQ.rearrange("p (h n) -> p h n", h=H)).then_inc(s_qe, 1)

                def a_dve(gi, first=False, last=False):
                    g = b * NG + gi
                    for t in range(TG):
                        n, at = g * TG + t, gi * TG + t
                        sums(n, at, t)
                        if t == 0 and not last:
                            group_stats(g + 1, gi + 1)
                        normal_qk(n, t)
                        if not (first and t < 1):
                            low_qk(n - 1, at - 1, t - 1)
                        if t == 0 and not last:
                            ln_a.begin(g + 1, 2 * TG)
                            group_normal(g + 1, gi + 1)
                        if t == 2 and not last:
                            low_y(g + 1)
                        if not (first and t < 2):
                            move_q(n - 2, at - 2)

                group_stats(b * NG, 0)
                group_normal(b * NG, 0)
                low_y(b * NG)
                groups(dve, a_dve)
                end = b * NT + NT
                low_qk(end - 1, NT - 1, NT - 1)
                move_q(end - 2, NT - 2)
                move_q(end - 1, NT - 1)
                wait(dve, s_qs, b * NT + NT)
                dve.tensor_reduce(qmx[:, :], qn2[:, :, :].rearrange("p t h -> p h t"), AX.X, ALU.max).then_inc(s_mxD, 1)
                wait(dve, s_mxT, b + 1)
                dve.tensor_reduce(qmT[:, :], bank(0)[0:H, 0:P], AX.X, ALU.max).then_inc(s_mxD, 1)
                wait(dve, s_mxD, 3 * b + 2)
                dve.tensor_scalar(qmD[:, :], ident[0:H, 0:H], qmT[:, 0:1], None, ALU.mult).then_inc(s_mxD, 1)
                wait(dve, s_mx, b + 1)
                dve.tensor_scalar(nbias[:, :], nm[:, 0:H], CESC, None, ALU.mult).then_inc(s_nb, 1)
                wait(dve, s_nb, 2 * b + 1)
                dve.tensor_scalar(nbias[:, :], nbias[:, :], -KSCALE * math.sqrt(DH), TOP, ALU.mult, ALU.add).then_inc(s_nb, 1)

                def parts(hh, h, k):
                    s = hh * STEPS + k
                    if not (isinstance(h, int) and k < NEP):
                        wait(dve, s_PV, s - NEP + 1)
                    if k in ACT_H:
                        wait(dve, s_EhA, hh * len(ACT_H) + act_h(k) + 1)
                    else:
                        wait(dve, s_E, s + 1)
                        dve.tensor_copy(e_h[:, k % NEP, :], e_f[:, k % NEF, :]).then_inc(s_EhD, 1)
                        wait(dve, s_EhD, hh * (STEPS - len(ACT_H)) + k - act_h(k) + 1)
                    dve.tensor_tensor(e_l[:, k % NEP, :], e_f[:, k % NEF, :], e_h[:, k % NEP, :], ALU.subtract).then_inc(s_El, 1)

                def sum_out(unit, local):
                    wait(dve, s_OL, unit + 1)
                    a = attn[:, bass.ds(local * QT, QT), :] if not isinstance(local, int) else attn[:, local * QT:local * QT + QT, :]
                    lv = lsum[:, bass.ds(local * QT, QT)] if not isinstance(local, int) else lsum[:, local * QT:local * QT + QT]
                    dve.tensor_tensor(a.rearrange("p (b q) d -> p b q d", q=2), ps_O[:, :, :, 0:DH],
                                      ov_l[:, :, :].rearrange("p (b q) d -> p b q d", q=2), ALU.add).then_inc(s_Oev, 1)
                    dve.tensor_copy(lv.rearrange("p (b q) -> p b q", q=2), ps_O[:, :, :, DH]).then_inc(s_Oev, 1)

                def head_dve(b, h):
                    hh = b * H + h
                    for k in range(STEPS):
                        if k % NT == LAG - 1 and not (isinstance(h, int) and k < NT):
                            u = k // NT - 1
                            sum_out(hh * NQB + u, h * NQB + u)
                        parts(hh, h, k)

                head_dve(b, 0)
                with dve.Fori(1, H) as h:
                    head_dve(b, h)
                sum_out(b * H * NQB + H * NQB - 1, H * NQB - 1)

                wait(dve, s_Oev, 2 * (b * H * NQB + H * NQB))
                dve.reciprocal(rl[:, :, :], lsum[:, :].rearrange("p (h t) -> p h t", h=H)).then_inc(s_rl, 1)
                wait(dve, s_rl, 2 * b + 1)
                dve.tensor_scalar(rl[:, :, :], rl[:, :, :], CIV, None, ALU.mult).then_inc(s_rl, 1)

                front = Chain(dve, s_c, 2 * (2 * TG + 1))
                last5 = Chain(dve, s_c5, 2 * TG + 1)
                y = y_f[:, :, :].rearrange("p k (t d) -> p (k t) d", d=D)

                def x_tile(gi, t):
                    return x_all[:, bass.ds(gi * TG + t, 1), :].rearrange("p o d -> p (o d)")

                def xe_tile(gi, t):
                    return xe[:, bass.ds(gi * TG + t, 1), :].rearrange("p o d -> p (o d)")

                def low_attention(g):
                    wait(dve, s_ah, g + 1)
                    dve.tensor_tensor(y_l[:, :, :], ps_T3, y_h[:, :, :].bitcast(f32), ALU.subtract).then_inc(s_al, 1)

                def variances(src):
                    for t in range(TG):
                        front.link(dve.bn_stats(st[:, t, :], src(t)))
                    front.follow()
                    dve.sem_inc(s_held, 1)
                    for t in range(TG):
                        front.link(dve.bn_aggr(mv[:, t, :], st[:, t, :]))
                    front.follow()
                    dve.tensor_scalar(var[:, :], mv[:, :, 1], LN_EPS, None, ALU.add).then_inc(s_var3, 1)

                def projected(g):
                    front.begin(g)
                    wait(dve, s_xa, g)
                    for i in range(2):
                        wait(dve, s_Y, 2 * g + i + 1)
                        dve.tensor_tensor(y[:, 2 * i:2 * i + 2, :], ps_Y[i].rearrange("p (t d) -> p t d", d=D),
                                          spread(bo_row[:, :], 1, 2), ALU.add).then_inc(s_yb, 1)
                    wait(dve, s_yb, 2 * g + 2)
                    variances(lambda t: y[:, t, :])

                def normal_y(g):
                    wait(dve, s_sd3, 2 * g + 1)
                    front.link(dve.reciprocal(rs[:, :], sd[:, :]))
                    front.follow()
                    for t in range(TG):
                        dve.tensor_scalar(y[:, t, :], y[:, t, :], mv[:, t, 0:1], rs[:, t:t + 1], ALU.subtract,
                                          ALU.mult).then_inc(s_yn, 1)

                def second_stats(g, gi):
                    wait(dve, s_xa, g + 1)
                    wait(dve, s_yn, g * TG + TG)
                    variances(lambda t: x_tile(gi, t))

                def normal_x(g, gi):
                    wait(dve, s_sd3, 2 * g + 2)
                    front.link(dve.reciprocal(rs[:, :], sd[:, :]))
                    front.follow()
                    wait(dve, s_T4, g)
                    wait(dve, s_xc, g)
                    for t in range(TG):
                        dve.tensor_scalar(xn[:, t, :], x_tile(gi, t), mv[:, t, 0:1], rs[:, t:t + 1], ALU.subtract,
                                          ALU.mult).then_inc(s_xn, 1)

                def low_n(g):
                    wait(dve, s_nh, g + 1)
                    dve.tensor_tensor(n_l[:, :, :], ps_T, n_h[:, :, :].bitcast(f32), ALU.subtract).then_inc(s_nl, 1)

                GATE = 6

                def choose(g):
                    own = Chain(dve, s_Gr, GATE)
                    own.begin(g)
                    bc = lambda a: spread(a, 2, NE)
                    rk = spread(rank[:, :], 1, TG)
                    wait(dve, s_G, g + 1)
                    wait(dve, s_Xr, g * TG * NE)
                    own.link(dve.tensor_copy(gs[:, :, :], ps_G.rearrange("p (t e) -> p t e", e=NE)))
                    own.follow()
                    own.link(dve.tensor_reduce(gm[:, :], gs[:, :, :], AX.X, ALU.max))
                    own.follow()
                    own.link(dve.tensor_tensor(hot[:, :, :], gs[:, :, :], bc(gm[:, :]), ALU.is_equal))
                    own.follow()
                    own.link(dve.tensor_tensor(hot[:, :, :], hot[:, :, :], rk, ALU.mult))
                    own.follow()
                    own.link(dve.tensor_reduce(gm[:, :], hot[:, :, :], AX.X, ALU.max))
                    own.follow()
                    own.link(dve.tensor_tensor(hot[:, :, :], rk, bc(gm[:, :]), ALU.is_equal))
                    own.follow()
                    assert own.n == GATE

                def select(g, gi, t):
                    m = (g * TG + t) * NE
                    if t == 0:
                        wait(dve, s_xc, g + 1)
                    for e in range(NE):
                        if e % 2 == 0:
                            wait(dve, s_X, (g * TG + t) * XR + e // 2 + 1)
                        if e >= 2:
                            wait(dve, s_Xr, m + e - 1)
                        src, w = ps_X[e // 2][:, (e % 2) * D:(e % 2) * D + D], hot[:, t, e:e + 1]
                        fb = f_b[:, t % 2, :]
                        if e == 1:
                            wait(dve, s_fs, g * TG + t - 1)
                            dve.tensor_scalar(fb, src, w, None, ALU.mult).then_inc(s_Xr, 1)
                        else:
                            a = xe_tile(gi, t) if e % 2 == 0 else fb
                            dve.scalar_tensor_tensor(out=a, in0=src, scalar=w, in1=a, op0=ALU.mult,
                                                     op1=ALU.add).then_inc(s_Xr, 1)

                def sum_stats(g, gi, t):
                    wait(dve, s_fs, g * TG + t + 1)
                    if t == 0:
                        last5.begin(g)
                    last5.link(dve.bn_stats(st5[:, t, :], xe_tile(gi, t)))

                def sum_variances(g):
                    last5.follow()
                    dve.sem_inc(s_held, 1)
                    for t in range(TG):
                        last5.link(dve.bn_aggr(mv5[:, t, :], st5[:, t, :]))
                    last5.follow()
                    dve.tensor_scalar(var5[:, :], mv5[:, :, 1], LN_EPS, None, ALU.add).then_inc(s_var5, 1)

                def normal_sum(g, gi):
                    wait(dve, s_sd5, g + 1)
                    last5.link(dve.reciprocal(rs5[:, :], sd5[:, :]))
                    last5.follow()
                    for t in range(TG):
                        dve.tensor_scalar(xe_tile(gi, t), xe_tile(gi, t), mv5[:, t, 0:1], rs5[:, t:t + 1], ALU.subtract,
                                          ALU.mult).then_inc(s_f5, 1)

                def c_dve(gi, first=False, last=False):
                    g = b * NG + gi
                    if not last:
                        low_attention(g + 1)
                    choose(g)
                    select(g, gi, 0)
                    if not first:
                        last5.begin(g - 1)
                        last5.n = TG - 1
                        sum_stats(g - 1, gi - 1, TG - 1)
                        sum_variances(g - 1)
                    if not last:
                        projected(g + 1)
                    select(g, gi, 1)
                    if not first:
                        normal_sum(g - 1, gi - 1)
                    if not last:
                        normal_y(g + 1)
                    sum_stats(g, gi, 0)
                    select(g, gi, 2)
                    if not last:
                        second_stats(g + 1, gi + 1)
                    sum_stats(g, gi, 1)
                    if not last:
                        normal_x(g + 1, gi + 1)
                    select(g, gi, 3)
                    sum_stats(g, gi, 2)
                    if not last:
                        low_n(g + 1)

                g0 = b * NG
                low_attention(g0)
                projected(g0)
                normal_y(g0)
                second_stats(g0, 0)
                normal_x(g0, 0)
                low_n(g0)
                groups(dve, c_dve)
                sum_stats(g0 + NG - 1, NG - 1, TG - 1)
                sum_variances(g0 + NG - 1)
                normal_sum(g0 + NG - 1, NG - 1)

        @block.tensor
        def _(pe):
            start_up(pe, "pe")
            def split_mm(dst, terms, start=True):
                n = len(terms)
                for i, (l, r) in enumerate(terms):
                    ins = pe.matmul(dst, l, r, start=(i == 0), stop=(i == n - 1))
                return ins

            wait(pe, s_ones, 1)
            wait(pe, s_prepA, 1)
            pe.matmul(bank(0)[:, 0:1], ones[:, :], part[:, 0:1], start=True, stop=True).then_inc(s_prepP, 1)
            wait(pe, s_id, 4)
            wait(pe, s_prep, 3)
            wait(pe, s_ws, 1)

            def transpose_group(g, done):
                for k in range(KH):
                    for t in range(TG):
                        ins = pe.transpose(ps_T[:, k, t * P:(t + 1) * P], xhat[:, t, k * P:(k + 1) * P], ident[:, :])
                ins.then_inc(done, 1)

            def three(t, w_h, w_l, c0, c1, a_h=y_h, a_l=y_l):
                tok = slice(t * P, (t + 1) * P)
                return [(a[:, k, tok], w[:, k, c0:c1]) for a, w in ((a_h, w_h), (a_l, w_h), (a_h, w_l)) for k in range(KH)]

            def project(n, t):
                wait(pe, s_qkn, n - 1)
                wait(pe, s_vl, n - 1)
                split_mm(ps_QK[t % 2], three(t % TG, wqkv_h, wqkv_l, 0, 2 * D))
                split_mm(ps_V[t % 2], three(t % TG, wqkv_h, wqkv_l, 2 * D, 3 * D)).then_inc(s_P, 1)

            def transpose_qk(n, t):
                qs = qk_s[t % 2]
                wait(pe, s_lo, n + 1)
                wait(pe, s_qe, n)
                wait(pe, s_ke, n)
                for h in range(H):
                    pe.transpose(ps_TQ[:, h * P:(h + 1) * P], qs[:, h, 0:2 * DH], ident16[:, :])
                for h in range(H):
                    for a in range(2):
                        ins = pe.transpose(ps_TK[:, (2 * h + a) * P:(2 * h + a + 1) * P],
                                           qs[:, H + h, a * DH:(a + 2) * DH], ident16[:, :])
                ins.then_inc(s_T2, 1)

            with pe.Fori(0, NB) as b:
                def group_T(g):
                    wait(pe, s_xh, g * TG + TG)
                    wait(pe, s_yh, KH * g)
                    transpose_group(g, s_T)

                def a_pe(gi, first=False, last=False):
                    g = b * NG + gi
                    for t in range(TG):
                        n = g * TG + t
                        if t < TG - 1 or not last:
                            if t == TG - 1:
                                wait(pe, s_ys, g + 2)
                            project(n + 1, t + 1)
                        if not (first and t < 1):
                            transpose_qk(n - 1, t - 1)
                        if t == 0 and not last:
                            group_T(g + 1)

                wait(pe, s_E, b * H * STEPS)
                group_T(b * NG)
                wait(pe, s_ys, b * NG + 1)
                project(b * NT, 0)
                groups(pe, a_pe)
                transpose_qk(b * NT + NT - 1, NT - 1)
                wait(pe, s_mxD, 3 * b + 1)
                pe.transpose(bank(0)[0:H, 0:P], qmx[:, :], ident[:, :]).then_inc(s_mxT, 1)
                wait(pe, s_mxD, 3 * b + 3)
                pe.matmul(bank(0)[:, 0:H], ones[0:H, :], qmD[:, :], start=True, stop=True).then_inc(s_mxB, 1)
                wait(pe, s_mx, b + 1)
                wait(pe, s_ke, b * NT + NT)
                wait(pe, s_qe, b * NT + NT)

                def scores(hh, h, k):
                    s = hh * STEPS + k
                    qb, j = k // NT, k % NT
                    first = isinstance(h, int)
                    if not (first and k < 2):
                        wait(pe, s_E, s - 1)
                    nc.disable_value_cache = False
                    for a in range(2):
                        if first:
                            kt = k_T[:, a, h * N + j * P:h * N + (j + 1) * P]
                        else:
                            kt = k_T[:, a, bass.ds(h * N + j * P, P)]
                        for c in range(QB // BANK):
                            at = qb * QB + c * BANK
                            qt = q_T[:, h * N + at:h * N + at + BANK] if first else q_T[:, bass.ds(h * N + at, BANK)]
                            ins = pe.matmul(ps_S[k % 2][:, c * BANK:(c + 1) * BANK], kt, qt, start=(a == 0), stop=(a == 1),
                                            skip_group_check=True)
                    nc.disable_value_cache = True
                    ins.then_inc(s_S, 1)

                def pv(hh, h, k, unit):
                    s = hh * STEPS + k
                    j = k % NT
                    wait(pe, s_El, s + 1)
                    if j == 0:
                        wait(pe, s_Oev, 2 * unit)
                    at = j * H + h
                    v = (lambda w: v_mm[:, at, 0:w]) if isinstance(at, int) else (
                        lambda w: v_mm[:, bass.ds(at, 1), 0:w].rearrange("p o w -> p (o w)"))
                    nc.disable_value_cache = False
                    for q in range(QT):
                        for e, w in ((e_h, VW), (e_l, DH + 1)):
                            ins = pe.matmul(ps_O[:, q // 2, q % 2, 0:w], e[:, k % NEP, q * P:(q + 1) * P], v(w),
                                            start=(j == 0 and q % 2 == 0 and w == VW), stop=(j == NT - 1 and w != VW),
                                            skip_group_check=True)
                    nc.disable_value_cache = True
                    ins.then_inc(s_PV, 1)

                def head_pe(b, h):
                    hh = b * H + h
                    for k in range(STEPS):
                        scores(hh, h, k)
                        if k >= LAG:
                            pv(hh, h, k - LAG, hh * NQB + (k - LAG) // NT)
                        elif not isinstance(h, int):
                            pv(hh - 1, h - 1, STEPS + k - LAG, hh * NQB - 1)

                head_pe(b, 0)
                with pe.Fori(1, H) as h:
                    head_pe(b, h)
                for k in range(STEPS - LAG, STEPS):
                    pv(b * H + H - 1, H - 1, k, b * H * NQB + H * NQB - 1)

                wait(pe, s_ws, 4)
                def attention_T(g):
                    wait(pe, s_at, g + 1)
                    wait(pe, s_yb, 2 * g)
                    for k in range(KH):
                        for t in range(TG):
                            ins = pe.transpose(ps_T3[:, k, t * P:(t + 1) * P],
                                               xa[:, t, k * P:(k + 1) * P], ident[:, :])
                    ins.then_inc(s_T3, 1)

                def project_attention(g):
                    wait(pe, s_al, g + 1)
                    for i in range(2):
                        for t in range(2 * i, 2 * i + 2):
                            ins = split_mm(ps_Y[i][:, (t % 2) * D:(t % 2 + 1) * D], three(t, wo_h, wo_l, 0, D))
                        ins.then_inc(s_Y, 1)

                def norm_T(g):
                    wait(pe, s_xn, g * TG + TG)
                    wait(pe, s_Gr, g * 6)
                    for k in range(KH):
                        for t in range(TG):
                            ins = pe.transpose(ps_T[:, k, t * P:(t + 1) * P],
                                               xn[:, t, k * P:(k + 1) * P], ident[:, :])
                    ins.then_inc(s_T4, 1)

                def gate(g):
                    wait(pe, s_nl, g + 1)
                    for t in range(TG):
                        ins = split_mm(ps_G[:, t * NE:(t + 1) * NE], three(t, wg_h, wg_l, 0, NE, n_h, n_l))
                    ins.then_inc(s_G, 1)

                def experts(g, t):
                    for c in range(XR):
                        wait(pe, s_Xr, (g * TG + t) * NE - NE + 2 * c + 2)
                        split_mm(ps_X[c], three(t, we_h, we_l, c * BANK, (c + 1) * BANK, n_h, n_l)).then_inc(s_X, 1)

                def c_pe(gi, last=False):
                    g = b * NG + gi
                    if not last:
                        attention_T(g + 1)
                    gate(g)
                    experts(g, 0)
                    if not last:
                        project_attention(g + 1)
                    for t in range(1, TG):
                        experts(g, t)
                    if not last:
                        norm_T(g + 1)

                wait(pe, s_E, (b * H + H) * STEPS)
                wait(pe, s_Oev, 2 * (b * H * NQB + H * NQB))
                attention_T(b * NG)
                project_attention(b * NG)
                norm_T(b * NG)
                with pe.Fori(0, NG - 1) as gi:
                    c_pe(gi)
                c_pe(NG - 1, last=True)


def kernel(**inputs):
    import numpy as np
    import concourse.bacc as bacc
    from concourse.bass_utils import run_bass_kernel_spmd

    def get(name):
        return np.asarray(inputs[name])

    we = get("L0_ffn_expert_w")
    arrays = {
        "x": get("L0_attn_x"),
        "wqkvT": np.concatenate([get("L0_attn_w_" + n).T for n in "qkv"], axis=1),
        "woT": get("L0_attn_w_o").T,
        "weT": we.transpose(2, 0, 1).reshape(we.shape[2], -1),
        "wgT": get("L0_ffn_gate_w").T,
        "ln_gamma": get("L0_attn_ln_gamma"),
        "ln_beta": get("L0_attn_ln_beta"),
        "q_gamma": get("L0_attn_q_gamma"),
        "k_gamma": get("L0_attn_k_gamma"),
        "b_o": get("L0_attn_b_o"),
    }
    arrays = {n: np.ascontiguousarray(a) for n, a in arrays.items()}
    nc = bacc.Bacc("TRN2", target_bir_lowering=False, num_devices=1)
    args = [nc.dram_tensor(n, a.shape, mybir.dt.from_np(a.dtype), kind="ExternalInput").ap() for n, a in arrays.items()]
    x = arrays["x"]
    out = nc.dram_tensor("out", x.shape, mybir.dt.from_np(x.dtype), kind="ExternalOutput").ap()
    build(nc, *args, out)
    return run_bass_kernel_spmd(nc, [arrays], core_ids=[0]).results[0]["out"]
```

```python
import math
from contextlib import ExitStack

import concourse.bass as bass
from concourse import mybir


def build(nc, x, wqkvT, woT, weT, wgT, ln_gamma, ln_beta, q_gamma, k_gamma, b_o, out):
    f32, f32r, f16, u32 = mybir.dt.float32, mybir.dt.float32r, mybir.dt.float16, mybir.dt.uint32
    ALU, ACT, AX = mybir.AluOpType, mybir.ActivationFunctionType, mybir.AxisListType
    P = 128
    NB, N, D = x.shape
    DH = q_gamma.shape[0]
    H = D // DH
    KH = D // P
    NE = wgT.shape[1]
    NT = N // P
    TG = 4
    NG = NT // TG
    QB = 1024
    NQB = N // QB
    QT = QB // P
    BANK = 512
    STEPS = NQB * NT
    LAG = 4
    NEF, NEP = 4, 4
    VW = DH + 1 + DH
    VS = VW + 1
    XR = 4
    BY_ACT = (2, 3)
    BY_DVE = [e for e in range(NE) if e not in BY_ACT]
    NX, NA = len(BY_DVE), len(BY_ACT)
    GATE = 6
    LN_EPS, RMS_EPS = 1e-5, 1e-8
    KSCALE = 32.0
    QMAX = 512.0
    TOP = 10.5

    nc.disable_value_cache = True
    with ExitStack() as ctx:
        def sb(name, shape, dt):
            return ctx.enter_context(nc.sbuf_tensor(name, shape, dt))

        def sem(name):
            return ctx.enter_context(nc.semaphore(name))

        x_all = sb("x_all", [P, NT, D], f32)
        wqkv_h, wqkv_l = (sb(n, [P, KH, 3 * D], f32r) for n in ("wqkv_h", "wqkv_l"))
        wo_h, wo_l = (sb(n, [P, KH, D], f32r) for n in ("wo_h", "wo_l"))
        we_h, we_l = (sb(n, [P, KH, NE * D], f32r) for n in ("we_h", "we_l"))
        wg_h, wg_l = (sb(n, [P, KH, NE], f32r) for n in ("wg_h", "wg_l"))
        q_T = sb("q_T", [P, H * N], f16)
        k_T = sb("k_T", [P, 2, H * N], f16)
        v_mm = sb("v_mm", [P, NT * H, VS], f16)
        attn = sb("attn", [P, H * NQB * QT, DH], f32)
        lsum = sb("lsum", [P, H * NQB * QT], f32)
        e_f = sb("e_f", [P, NEF, QB], f32)
        e_h, e_l = (sb(n, [P, NEP, QB], f16) for n in ("e_h", "e_l"))
        ov = sb("ov", [P, QT, VW], f32)
        y_h, y_l = (sb(n, [P, KH, TG * P], f32r) for n in ("y_h", "y_l"))
        n_h, n_l = (sb(n, [P, KH, TG * P], f32r) for n in ("n_h", "n_l"))
        e_f32 = e_f[:, :, :].rearrange("p s n -> p (s n)")
        y_f = e_f32[:, 0:KH * TG * P].rearrange("p (k n) -> p k n", k=KH)
        sq = [e_f32[:, (2 + i) * 2 * D:(3 + i) * 2 * D] for i in range(2)]
        e_l16 = e_l[:, :, :].rearrange("p s n -> p (s n)")
        qk_n = [e_l16[:, i * 4 * D:(i + 1) * 4 * D].bitcast(f32) for i in range(2)]
        e_h16 = e_h[:, :, :].rearrange("p s n -> p (s n)")
        xhat = e_h16[:, 0:2 * TG * D].bitcast(f32).rearrange("p (t d) -> p t d", d=D)
        qk_s = [a[:, 2048:2048 + 6 * H * DH].rearrange("p (h c) -> p h c", h=2 * H)
                for a in (e_h16, e_l16)]
        q_sq = e_h16[:, 3584:3584 + 2 * D].bitcast(f32)
        k32 = k_T[:, :, :].rearrange("p a n -> p (a n)").bitcast(f32)
        q32 = q_T[:, :].bitcast(f32)
        xa = q32[:, 0:TG * D].rearrange("p (t d) -> p t d", d=D)
        g_T = q32[0:NE, TG * D:TG * (D + P)]
        xe = k32[:, 0:NT * D].rearrange("p (t d) -> p t d", d=D)
        f_b, f_c = (k32[:, (NT + i) * D:(NT + i + 2) * D].rearrange("p (i d) -> p i d", d=D)
                    for i in (0, 2))
        splits = ((y_h, y_l), (n_h, n_l))
        ident = sb("ident", [P, P], f32)
        ident16 = sb("ident16", [P, P], f16)
        ones = sb("ones", [P, P], f32)
        gam, bet = (sb(n, [P, KH], f32) for n in ("gam", "bet"))
        gam_row, bet_row = (e_f32[:, i * D:(i + 1) * D] for i in range(2))
        bo_row = sb("bo_row", [P, D], f32)
        qg_row, kg_row = (sb(n, [P, DH], f32) for n in ("qg_row", "kg_row"))
        gq = sb("gq", [P, DH], f32)
        c_ = sb("c_", [P, 24], f32)
        part = sb("part", [P, 4], f32)
        st = sb("st", [P, TG, 6], f32)
        mv = sb("mv", [P, TG, 2], f32)
        var, sd, rs = (sb(n, [P, TG], f32) for n in ("var", "sd", "rs"))
        ss, nr, nm, rn = (sb(n, [P, 2 * H], f32) for n in ("ss", "nr", "nm", "rn"))
        warm = sb("warm", [P, 1], f32)
        rcol = sb("rcol", [P, 2 * H], f32)
        qn2 = sb("qn2", [P, NT, H], f32)
        qmx = sb("qmx", [P, H], f32)
        qmT = sb("qmT", [H, 1], f32)
        qmD = sb("qmD", [H, H], f32)
        nbias = sb("nbias", [P, H], f32)
        rl = sb("rl", [P, H * NT], f32)
        gs = sb("gs", [P, TG, NE], f32)
        gm = sb("gm", [P, TG], f32)
        hot = sb("hot", [P, TG, NE], f32)
        rank = sb("rank", [P, NE], f32)
        st5 = sb("st5", [P, TG, 6], f32)
        mv5 = sb("mv5", [P, TG, 2], f32)
        var5, sd5, rs5, nb5 = (sb(n, [P, TG], f32) for n in ("var5", "sd5", "rs5", "nb5"))

        banks = ctx.enter_context(nc.psum_tensor("banks", [P, 8 * BANK], f32))

        def bank(i, n=1):
            return banks[:, i * BANK:(i + n) * BANK]

        ps_S = [bank(0, 2), bank(2, 2)]
        ps_O = bank(4, 4).rearrange("p (b c) -> p b c", c=BANK)[:, :, 0:2 * VW].rearrange(
            "p b (q c) -> p b q c", c=VW)
        ps_T = bank(0, 2).rearrange("p (k c) -> p k c", k=KH)
        ps_QK = [bank(2), bank(3)]
        ps_V = [bank(4)[:, 0:D], bank(5)[:, 0:D]]
        ps_TQ = bank(6).bitcast(f16)[:, 0:H * P]
        ps_TK = bank(7).bitcast(f16)[:, 0:2 * H * P]
        ps_X = [bank(2 + i) for i in range(XR)]
        ps_Y = [[bank(i + (2 if gi == 0 else 6)) for i in range(2)] for gi in range(NG)]
        ps_T3 = [bank(0 if gi == 0 else 6, 2).rearrange("p (k c) -> p k c", k=KH) for gi in range(NG)]
        ps_GT = bank(0)[0:NE, :]
        ps_G = bank(1)[:, 0:TG * NE]

        raw_we = attn[:, :, :].rearrange("p t d -> p (t d)").rearrange("p (k n) -> p k n", k=KH)
        raw_q = q_T[:, :].bitcast(f32)
        raw_wqkv = raw_q[:, 0:KH * 3 * D].rearrange("p (k n) -> p k n", k=KH)
        raw_wo = raw_q[:, KH * 3 * D:KH * 4 * D].rearrange("p (k n) -> p k n", k=KH)
        raw_wg = sb("raw_wg", [P, KH, NE], f32)

        CQ, CESC, CV, CIV = (c_[:, i:i + 1] for i in range(4))
        tmp = [c_[:, i:i + 1] for i in range(4, 16)]

        owned = {}

        def sems(owner, names, first=2):
            made = [sem("s_" + n) for n in names.split()]
            owned.setdefault(owner, []).extend((m, first) for m in made)
            return made

        def start_of(s):
            return next((first for group in owned.values() for m, first in group if m is s), 0)

        def wait(eng, s, value):
            eng.wait_ge(s, value + start_of(s))

        def start_up(eng, owner):
            for s, first in owned.get(owner, []):
                eng.sem_inc(s, first)

        s_x, s_small, s_wq, s_wo, s_we, s_out = (sem("s_" + n) for n in "x small wq wo we out".split())
        s_id, s_rank, s_ones, s_wf, s_qg, s_q2 = sems("pool", "id rank ones wf qg q2")
        s_att, s_sum, s_at, s_xa, s_fa, s_fs, s_fin = sems("pool", "att sum at xa fa fs fin")
        s_prep, s_const, s_ws = sems("dve", "prep const ws")
        s_dve, s_dq, s_var, s_xh, s_ys, s_ss, s_qkn, s_lo, s_vl, s_qe, s_qs, s_mxD, s_nb = sems(
            "dve", "dve dq var xh ys ss qkn lo vl qe qs mxD nb")
        s_held, = sems("dve", "held")
        s_EhD, s_El, s_Oev = sems("dve", "EhD El Oev")
        s_c, s_rl, s_al, s_yb, s_var3, s_yn, s_xn, s_nl, s_Gr, s_c5, s_var5, s_nb5 = sems(
            "dve", "c rl al yb var3 yn xn nl Gr c5 var5 nb5")
        s_Xr, = sems("dve", "Xr", NX + 1)
        s_prepA, s_wh, s_sd, s_y, s_yh, s_sq, s_vh, s_nr, s_hi, s_ke, s_mx = sems("act", "prepA wh sd y yh sq vh nr hi ke mx")
        s_E, s_EhA, s_ah, s_sd3, s_nh, s_sd5, s_f5, s_XA, s_gT = sems("act", "E EhA ah sd3 nh sd5 f5 XA gT")
        s_prepP, s_T, s_P, s_T2, s_mxT, s_mxB = sems("pe", "prepP T P T2 mxT mxB")
        s_S, s_PV, s_T3, s_Y, s_T4, s_GT, s_G, s_X = sems("pe", "S PV T3 Y T4 GT G X")

        x_d = x.rearrange("b (t p) d -> p (b t) d", p=P)
        out_d = out.rearrange("b (t p) d -> p (b t) d", p=P)

        def spread(ap, axis, n):
            ap = ap.unsqueeze(axis)
            shape = list(ap.shape)
            shape[axis] = n
            return ap.to_broadcast(shape)

        def groups(eng, body):
            body(0, first=True)
            with eng.Fori(1, NG - 1) as gi:
                body(gi)
            body(NG - 1, last=True)

        class Chain:
            def __init__(self, eng, s, per):
                self.eng, self.s, self.per = eng, s, per

            def begin(self, g, n=0):
                self.g, self.n = g, n

            def link(self, ins):
                ins.then_inc(self.s, 1)
                self.n += 1
                assert self.n <= self.per

            def follow(self):
                wait(self.eng, self.s, self.g * self.per + self.n)

        ACT_H = [k for k in range(STEPS) if k % 2 == 0]

        def act_h(k):
            return sum(j < k for j in ACT_H)

        block = ctx.enter_context(nc.Block())

        @block.sync
        def _(sp):
            sp.dma_start(x_all[:, 0:TG, :], x_d[:, 0:TG, :]).then_inc(s_x, 16)
            sp.dma_start(raw_wqkv, wqkvT.rearrange("(k p) n -> p k n", p=P)).then_inc(s_wq, 16)
            sp.dma_start(raw_wo, woT.rearrange("(k p) n -> p k n", p=P)).then_inc(s_wo, 16)
            with sp.Fori(1, NG) as gi:
                wait(sp, s_x, gi * 16)
                sp.dma_start(x_all[:, bass.ds(gi * TG, TG), :], x_d[:, bass.ds(gi * TG, TG), :]).then_inc(s_x, 16)

            def store(b, gi):
                g = b * NG + gi
                wait(sp, s_fin, g + 1)
                sp.dma_start(out_d[:, bass.ds(g * TG, TG), :], x_all[:, bass.ds(gi * TG, TG), :]).then_inc(s_out, 16)

            with sp.Fori(0, NB - 1) as b:
                with sp.Fori(0, NG) as gi:
                    store(b, gi)
                    g = b * NG + gi
                    wait(sp, s_out, (g + 1) * 16)
                    wait(sp, s_x, (g + NG) * 16)
                    sp.dma_start(x_all[:, bass.ds(gi * TG, TG), :], x_d[:, bass.ds((g + NG) * TG, TG), :]).then_inc(s_x, 16)
            with sp.Fori(0, NG) as gi:
                store(NB - 1, gi)
            wait(sp, s_out, NB * NG * 16)

        @block.gpsimd
        def _(pool):
            start_up(pool, "pool")
            for m in (ident, ident16):
                pool.memset(m[:, :], 0.0).then_inc(s_id, 1)
            pool.memset(ones[:, :], 1.0).then_inc(s_ones, 1)
            for e in range(NE):
                pool.memset(rank[:, e:e + 1], float(NE - e)).then_inc(s_rank, 1)
            for i in range(2 * H):
                pool.memset(rcol[:, i:i + 1], 1.0 if i < H else 1.0 / KSCALE).then_inc(s_rank, 1)
            pool.memset(v_mm[:, :, DH:DH + 1], 1.0).then_inc(s_ones, 1)
            wait(pool, s_id, 2)
            for m in (ident, ident16):
                pool.affine_select(out=m[:, :], in_=m[:, :], compare_op=ALU.not_equal, fill=1.0, base=0,
                                   pattern=[[-1, P]], channel_multiplier=1).then_inc(s_id, 1)
            for i, (w, hi, lo) in enumerate(((raw_wo, wo_h, wo_l), (raw_wg[:, :, :], wg_h, wg_l))):
                wait(pool, s_wh, i + 2)
                pool.tensor_tensor(lo[:, :, :], w, hi[:, :, :].bitcast(f32), ALU.subtract).then_inc(s_wf, 1)
            wait(pool, s_we, 16)
            pool.tensor_copy(we_h[:, :, :], raw_we).then_inc(s_wf, 1)
            wait(pool, s_wf, 3)
            pool.tensor_tensor(we_l[:, :, :], raw_we, we_h[:, :, :].bitcast(f32), ALU.subtract).then_inc(s_wf, 1)
            wait(pool, s_const, 1)
            with pool.Fori(0, NB) as b:
                with pool.Fori(0, NG) as gi:
                    for t in range(TG):
                        n = (b * NG + gi) * TG + t
                        qn = qk_n[t % 2][:, 0:D]
                        qv = qn.rearrange("p (h d) -> p h d", h=H)
                        wait(pool, s_qkn, n + 1)
                        pool.tensor_tensor(qv, qv, spread(gq[:, :], 1, H), ALU.mult).then_inc(s_qg, 1)
                        wait(pool, s_qg, n + 1)
                        wait(pool, s_qs, n)
                        pool.tensor_tensor(q_sq[:, :], qn, qn, ALU.mult).then_inc(s_q2, 1)

                def unit_sums(u):
                    unit = b * H * NQB + u
                    wait(pool, s_Oev, 2 * unit + 2)
                    pool.tensor_tensor(attn[:, bass.ds(u * QT, QT), :], ov[:, :, 0:DH], ov[:, :, DH + 1:], ALU.add).then_inc(s_att, 1)
                    pool.tensor_copy(lsum[:, bass.ds(u * QT, QT)], ov[:, :, DH]).then_inc(s_sum, 1)

                with pool.Fori(0, H * NQB - 1) as u:
                    unit_sums(u)

                def tiles(gi, n=TG, t=0):
                    return slice(gi * TG + t, gi * TG + t + n)

                def normalise(gi):
                    wait(pool, s_T3, b * NG + gi)
                    pool.tensor_tensor(xa.rearrange("p t (h d) -> p h t d", h=H),
                                       attn[:, :, :].rearrange("p (h t) d -> p h t d", h=H)[:, :, tiles(gi), :],
                                       spread(rl[:, :].rearrange("p (h t) -> p h t", h=H)[:, :, tiles(gi)], 3, DH), ALU.mult).then_inc(s_at, 1)

                def residual(gi):
                    g = b * NG + gi
                    y = y_f[:, :, :].rearrange("p k (t d) -> p (k t) d", d=D)
                    for i in range(2):
                        wait(pool, s_yn, g * TG + 2 * i + 2)
                        xg = x_all[:, tiles(gi, 2, 2 * i), :]
                        pool.tensor_tensor(xg, xg, y[:, 2 * i:2 * i + 2, :], ALU.add).then_inc(s_xa, 1)

                def expert_sum(gi, t):
                    n = (b * NG + gi) * TG + t
                    xt = xe[:, gi * TG + t, :]
                    wait(pool, s_Xr, n * NX + NX)
                    wait(pool, s_T4, b * NG + gi + 1)
                    pool.tensor_tensor(xt, xt, f_b[:, t % 2, :], ALU.add).then_inc(s_fa, 1)
                    wait(pool, s_fa, n + 1)
                    pool.tensor_tensor(xt, xt, f_c[:, t % 2, :], ALU.add).then_inc(s_fs, 1)

                def finish(gi):
                    g = b * NG + gi
                    wait(pool, s_f5, g * TG + TG)
                    pool.tensor_tensor(x_all[:, tiles(gi), :], x_all[:, tiles(gi), :], xe[:, tiles(gi), :], ALU.add).then_inc(s_fin, 1)

                units = b * H * NQB + H * NQB
                wait(pool, s_rl, 2 * (units - 1))
                wait(pool, s_att, units - 1)
                wait(pool, s_S, (b * H + H - 1) * STEPS)
                normalise(0)
                normalise(1)
                unit_sums(H * NQB - 1)
                residual(0)
                wait(pool, s_rl, 2 * units)
                wait(pool, s_att, units)
                for gi in range(NG):
                    if gi + 2 < NG:
                        normalise(gi + 2)
                    if gi + 1 < NG:
                        residual(gi + 1)
                    for t in range(2):
                        expert_sum(gi, t)
                    if gi:
                        finish(gi - 1)
                    for t in range(2, TG):
                        expert_sum(gi, t)
                finish(NG - 1)

        @block.scalar
        def _(act):
            start_up(act, "act")
            for col, src in ((gam, ln_gamma), (bet, ln_beta)):
                for k in range(KH):
                    act.dma_start(col[:, k:k + 1], src[k * P:(k + 1) * P].rearrange("(p o) -> p o", o=1)).then_inc(s_small, 16)
            for dst, src in ((gam_row, ln_gamma), (bet_row, ln_beta), (bo_row, b_o), (qg_row, q_gamma), (kg_row, k_gamma)):
                act.dma_start(dst[:, :], src.partition_broadcast(P)).then_inc(s_small, 16)
            act.dma_start(raw_wg[:, :, :], wgT.rearrange("(k p) n -> p k n", p=P)).then_inc(s_small, 16)
            act.dma_start(raw_we, weT.rearrange("(k p) n -> p k n", p=P)).then_inc(s_we, 16)
            wait(act, s_ones, 1)
            act.activation(warm[:, :], ones[:, 0:1], ACT.Sqrt).then_inc(s_prepA, 1)
            wait(act, s_wq, 16)
            act.activation(xhat[:, 0:KH, :], raw_wqkv[:, :, 2 * D:3 * D], ACT.Square, accum_out=part[:, 0:1]).then_inc(s_prepA, 1)
            wait(act, s_small, 160)
            act.activation(sq[0][:, 0:D], gam_row, ACT.Square, accum_out=part[:, 1:2]).then_inc(s_prepA, 1)
            act.activation(sq[0][:, D:2 * D], bet_row, ACT.Square, accum_out=part[:, 2:3]).then_inc(s_prepA, 1)
            act.activation(wqkv_h[:, :, :], raw_wqkv, ACT.Copy).then_inc(s_wh, 1)
            wait(act, s_wo, 16)
            act.activation(wo_h[:, :, :], raw_wo, ACT.Copy).then_inc(s_wh, 1)
            act.activation(wg_h[:, :, :], raw_wg[:, :, :], ACT.Copy).then_inc(s_wh, 1)
            wait(act, s_prep, 6)
            act.activation(tmp[7], tmp[6], ACT.Sqrt).then_inc(s_prepA, 1)

            with act.Fori(0, NB) as b:
                def root(g):
                    wait(act, s_var, g + 1)
                    act.activation(sd[:, :], var[:, :], ACT.Sqrt).then_inc(s_sd, 1)

                def affine(g, dst, done):
                    for k in range(KH):
                        act.activation(dst[:, k, :], ps_T[:, k, :], ACT.Identity, bias=bet[:, k:k + 1],
                                       scale=gam[:, k:k + 1]).then_inc(done, 1)

                def whole_y(g):
                    wait(act, s_T, g + 1)
                    wait(act, s_ys, g)
                    affine(g, y_f, s_y)

                def high_y(g):
                    wait(act, s_P, g * TG)
                    affine(g, y_h, s_yh)

                def squares(n, at, t):
                    wait(act, s_P, n + 1)
                    wait(act, s_ss, n - 1)
                    act.activation(sq[t % 2], ps_QK[t % 2], ACT.Square).then_inc(s_sq, 1)
                    act.activation(v_mm[:, bass.ds(at * H, H), 0:DH], ps_V[t % 2].rearrange("p (h d) -> p h d", h=H),
                                   ACT.Copy, scale=CV).then_inc(s_vh, 1)

                def norms(n):
                    wait(act, s_ss, n + 1)
                    act.activation(nr[:, :], ss[:, :], ACT.Sqrt, scale=1.0 / DH).then_inc(s_nr, 1)

                def high_qk(n, t):
                    qn, qs = qk_n[t % 2], qk_s[t % 2]
                    wait(act, s_qg, n + 1)
                    wait(act, s_T2, n - 1)
                    act.activation(qs[:, :, 0:DH], qn.rearrange("p (h d) -> p h d", d=DH), ACT.Copy).then_inc(s_hi, 1)
                    act.activation(qs[:, H:, 2 * DH:], qn[:, D:].rearrange("p (h d) -> p h d", d=DH), ACT.Copy).then_inc(s_hi, 1)

                def move_k(n, at):
                    wait(act, s_T2, n + 1)
                    act.activation(k_T[:, :, :].rearrange("p a (h n) -> p h a n", h=H)[:, :, :, bass.ds(at * P, P)],
                                   ps_TK.rearrange("p (h a n) -> p h a n", h=H, a=2), ACT.Copy).then_inc(s_ke, 1)

                def a_act(gi, first=False, last=False):
                    g = b * NG + gi
                    for t in range(TG):
                        n, at = g * TG + t, gi * TG + t
                        squares(n, at, t)
                        if not (first and t < 1):
                            high_qk(n - 1, t - 1)
                        norms(n)
                        if t == 0 and not last:
                            root(g + 1)
                        if t == 2 and not last:
                            high_y(g + 1)
                        if not (first and t < 2):
                            move_k(n - 2, at - 2)
                        if t == 1 and not last:
                            whole_y(g + 1)

                root(b * NG)
                whole_y(b * NG)
                high_y(b * NG)
                groups(act, a_act)
                end = b * NT + NT
                high_qk(end - 1, NT - 1)
                move_k(end - 2, NT - 2)
                move_k(end - 1, NT - 1)
                wait(act, s_mxB, b + 1)
                act.activation(nm[:, 0:H], bank(0)[:, 0:H], ACT.Sqrt).then_inc(s_mx, 1)
                wait(act, s_nb, 2 * b + 2)

                def exp_step(hh, h, k):
                    s = hh * STEPS + k
                    wait(act, s_S, s + 1)
                    if not (isinstance(h, int) and k < NEF):
                        wait(act, s_El, s - NEF + 1)
                    act.activation(e_f[:, k % NEF, :], ps_S[k % 2], ACT.Exp, bias=bias_of(h), scale=CESC).then_inc(s_E, 1)
                    j = k - 1
                    if j in ACT_H:
                        if not (isinstance(h, int) and j < NEP):
                            wait(act, s_PV, s - NEP)
                        wait(act, s_E, s)
                        act.activation(e_h[:, j % NEP, :], e_f[:, j % NEF, :], ACT.Copy).then_inc(s_EhA, 1)

                def bias_of(h):
                    return nbias[:, h:h + 1] if isinstance(h, int) else nbias[:, bass.ds(h, 1)]

                def head_act(b, h):
                    hh = b * H + h
                    for k in range(STEPS):
                        exp_step(hh, h, k)

                head_act(b, 0)
                with act.Fori(1, H) as h:
                    head_act(b, h)

                def high_attention(g, gi):
                    wait(act, s_T3, g + 1)
                    if gi >= 2:
                        wait(act, s_X, (g - 1) * TG * XR)
                    act.activation(splits[gi % 2][0][:, :, :], ps_T3[gi], ACT.Copy).then_inc(s_ah, 1)

                def root3(g, i):
                    wait(act, s_var3, 2 * g + i + 1)
                    act.activation(sd[:, :], var[:, :], ACT.Sqrt).then_inc(s_sd3, 1)

                def high_n(g, gi):
                    wait(act, s_T4, g + 1)
                    wait(act, s_Y, 2 * g + 2)
                    act.activation(splits[gi % 2][0][:, :, :], ps_T, ACT.Copy).then_inc(s_nh, 1)

                def move_gate(g):
                    wait(act, s_GT, g + 1)
                    wait(act, s_G, g)
                    act.activation(g_T, ps_GT, ACT.Copy).then_inc(s_gT, 1)

                def weigh(g, t):
                    n = g * TG + t
                    if t == 0:
                        wait(act, s_Gr, (g + 1) * GATE)
                    wait(act, s_fs, n - 1)
                    for e, f in zip(BY_ACT, (f_c, f_b)):
                        wait(act, s_X, n * XR + e // 2 + 1)
                        act.activation(f[:, t % 2, :], ps_X[e // 2][:, (e % 2) * D:(e % 2) * D + D], ACT.Copy,
                                       scale=hot[:, t, e:e + 1]).then_inc(s_XA, 1)

                def root5(g):
                    wait(act, s_var5, g + 1)
                    act.activation(sd5[:, :], var5[:, :], ACT.Sqrt).then_inc(s_sd5, 1)

                def normal_sums(g, gi):
                    wait(act, s_nb5, g + 1)
                    for t in range(TG):
                        xt = xe[:, gi * TG + t, :]
                        act.activation(xt, xt, ACT.Identity, bias=nb5[:, t:t + 1], scale=rs5[:, t:t + 1]).then_inc(s_f5, 1)

                g0 = b * NG
                high_attention(g0, 0)
                root3(g0, 0)
                high_attention(g0 + 1, 1)
                root3(g0, 1)
                high_n(g0, 0)
                for gi in range(NG):
                    g, more = g0 + gi, gi + 1 < NG
                    if more and gi:
                        high_attention(g + 1, gi + 1)
                    move_gate(g)
                    weigh(g, 0)
                    if more:
                        root3(g + 1, 0)
                    if gi:
                        root5(g - 1)
                    weigh(g, 1)
                    if more:
                        root3(g + 1, 1)
                    if gi:
                        normal_sums(g - 1, gi - 1)
                    weigh(g, 2)
                    weigh(g, 3)
                    if more:
                        high_n(g + 1, gi + 1)
                root5(g0 + NG - 1)
                normal_sums(g0 + NG - 1, NG - 1)

        @block.vector
        def _(dve):
            start_up(dve, "dve")
            wait(dve, s_prepP, 1)
            wait(dve, s_prepA, 4)
            dve.tensor_scalar(tmp[4], part[:, 1:2], float(D), None, ALU.mult).then_inc(s_prep, 1)
            wait(dve, s_prep, 1)
            dve.tensor_tensor(tmp[5], tmp[4], part[:, 2:3], ALU.add).then_inc(s_prep, 1)
            wait(dve, s_prep, 2)
            dve.tensor_scalar(tmp[8], bank(0)[:, 0:1], 2.0, None, ALU.mult).then_inc(s_prep, 1)
            wait(dve, s_prep, 3)
            dve.tensor_tensor(tmp[9], tmp[5], tmp[8], ALU.mult).then_inc(s_prep, 1)
            wait(dve, s_prep, 4)
            dve.tensor_scalar(tmp[10], tmp[9], 1e-30, None, ALU.max).then_inc(s_prep, 1)
            wait(dve, s_prep, 5)
            dve.tensor_scalar(tmp[6], tmp[10], 2.0 ** -28, None, ALU.mult).then_inc(s_prep, 1)
            wait(dve, s_wh, 1)
            dve.tensor_tensor(wqkv_l[:, :, :], raw_wqkv, wqkv_h[:, :, :].bitcast(f32), ALU.subtract).then_inc(s_ws, 1)
            wait(dve, s_small, 160)
            dve.tensor_tensor(gq[:, :], qg_row[:, :], kg_row[:, :], ALU.mult).then_inc(s_prep, 1)
            wait(dve, s_prep, 7)
            dve.tensor_reduce(tmp[0], gq[:, :], AX.X, ALU.max, apply_absolute_value=True).then_inc(s_prep, 1)
            wait(dve, s_prep, 8)
            dve.tensor_scalar(tmp[1], tmp[0], 1e-30, 1.0 / QMAX, ALU.max, ALU.mult).then_inc(s_prep, 1)
            wait(dve, s_prep, 9)
            dve.reciprocal(tmp[2], tmp[1]).then_inc(s_prep, 1)
            wait(dve, s_prepA, 5)
            dve.reciprocal(tmp[11], tmp[7]).then_inc(s_prep, 1)
            wait(dve, s_prep, 11)
            dve.tensor_scalar(CQ.bitcast(u32), tmp[2].bitcast(u32), 0x7F800000, None, ALU.bitwise_and).then_inc(s_prep, 1)
            dve.tensor_scalar(CV.bitcast(u32), tmp[11].bitcast(u32), 0x7F800000, None, ALU.bitwise_and).then_inc(s_prep, 1)
            wait(dve, s_prep, 13)
            dve.reciprocal(CIV, CV).then_inc(s_prep, 1)
            dve.reciprocal(tmp[3], CQ).then_inc(s_prep, 1)
            wait(dve, s_prep, 15)
            dve.tensor_scalar(CESC, tmp[3], 1.0 / (KSCALE * math.sqrt(DH)), None, ALU.mult).then_inc(s_prep, 1)
            wait(dve, s_prep, 16)
            dve.tensor_scalar(gq[:, :], gq[:, :], CQ, None, ALU.mult).then_inc(s_const, 1)
            wait(dve, s_rank, NE + 2 * H)
            ln_a = Chain(dve, s_dve, 2 * TG + 1)
            qk_a = Chain(dve, s_dq, 2)
            with dve.Fori(0, NB) as b:
                def group_stats(g, gi):
                    wait(dve, s_x, g * 16 + 16)
                    ln_a.begin(g)
                    for t in range(TG):
                        ln_a.link(dve.bn_stats(st[:, t, :], x_all[:, bass.ds(gi * TG + t, 1), :]))
                    ln_a.follow()
                    dve.sem_inc(s_held, 1)
                    for t in range(TG):
                        ln_a.link(dve.bn_aggr(mv[:, t, :], st[:, t, :]))
                    ln_a.follow()
                    dve.tensor_scalar(var[:, :], mv[:, :, 1], 1.0 + LN_EPS, LN_EPS ** 2, ALU.mult, ALU.add).then_inc(s_var, 1)

                def group_normal(g, gi):
                    wait(dve, s_sd, g + 1)
                    ln_a.link(dve.reciprocal(rs[:, :], sd[:, :]))
                    ln_a.follow()
                    wait(dve, s_T, g)
                    for t in range(TG):
                        dve.tensor_scalar(xhat[:, t, :], x_all[:, bass.ds(gi * TG + t, 1), :].rearrange("p o d -> p (o d)"),
                                          mv[:, t, 0:1], rs[:, t:t + 1], ALU.subtract, ALU.mult).then_inc(s_xh, 1)

                def low_y(g):
                    wait(dve, s_yh, KH * g + KH)
                    wait(dve, s_P, g * TG)
                    dve.tensor_tensor(y_l[:, :, :], y_f[:, :, :], y_h[:, :, :].bitcast(f32), ALU.subtract).then_inc(s_ys, 1)

                def sums(n, at, t):
                    wait(dve, s_sq, n + 1)
                    dve.tensor_reduce(ss[:, :], sq[t % 2].rearrange("p (h d) -> p h d", d=DH), AX.X, ALU.add).then_inc(s_ss, 1)
                    wait(dve, s_vh, n + 1)
                    v = v_mm[:, bass.ds(at * H, H), :]
                    dve.scalar_tensor_tensor(out=v[:, :, DH + 1:VW], in0=ps_V[t % 2].rearrange("p (h d) -> p h d", h=H),
                                             scalar=CV, in1=v[:, :, 0:DH], op0=ALU.mult, op1=ALU.subtract).then_inc(s_vl, 1)

                def normal_qk(n, t):
                    wait(dve, s_nr, n + 1)
                    qk_a.begin(n)
                    qk_a.link(dve.scalar_tensor_tensor(out=nm[:, :], in0=nr[:, :], scalar=RMS_EPS, in1=rcol[:, :],
                                                       op0=ALU.max, op1=ALU.mult))
                    qk_a.follow()
                    qk_a.link(dve.reciprocal(rn[:, :], nm[:, :]))
                    qk_a.follow()
                    wait(dve, s_lo, n - 1)
                    wait(dve, s_hi, 2 * n - 2)
                    wait(dve, s_q2, n - 1)
                    dve.tensor_tensor(qk_n[t % 2].rearrange("p (h d) -> p h d", d=DH),
                                      ps_QK[t % 2].rearrange("p (h d) -> p h d", d=DH),
                                      spread(rn[:, :], 2, DH), ALU.mult).then_inc(s_qkn, 1)

                def low_qk(n, at, t):
                    wait(dve, s_hi, 2 * n + 2)
                    qs = qk_s[t % 2]
                    dve.tensor_tensor(qs[:, :, DH:2 * DH], qk_n[t % 2].rearrange("p (h d) -> p h d", d=DH),
                                      qs[:, :, 0:DH], ALU.subtract).then_inc(s_lo, 1)
                    wait(dve, s_q2, n + 1)
                    dve.tensor_reduce(qn2[:, bass.ds(at, 1), :].rearrange("p o h -> p (o h)"),
                                      q_sq[:, :].rearrange("p (h d) -> p h d", d=DH), AX.X, ALU.add).then_inc(s_qs, 1)

                def move_q(n, at):
                    wait(dve, s_T2, n + 1)
                    dve.tensor_copy(q_T[:, :].rearrange("p (h n) -> p h n", h=H)[:, :, bass.ds(at * P, P)],
                                    ps_TQ.rearrange("p (h n) -> p h n", h=H)).then_inc(s_qe, 1)

                def a_dve(gi, first=False, last=False):
                    g = b * NG + gi
                    for t in range(TG):
                        n, at = g * TG + t, gi * TG + t
                        sums(n, at, t)
                        if not (first and t < 2):
                            move_q(n - 2, at - 2)
                        if t == 0 and not last:
                            group_stats(g + 1, gi + 1)
                        normal_qk(n, t)
                        if not (first and t < 1):
                            low_qk(n - 1, at - 1, t - 1)
                        if t == 0 and not last:
                            ln_a.begin(g + 1, 2 * TG)
                            group_normal(g + 1, gi + 1)
                        if t == 2 and not last:
                            low_y(g + 1)

                group_stats(b * NG, 0)
                group_normal(b * NG, 0)
                low_y(b * NG)
                groups(dve, a_dve)
                end = b * NT + NT
                low_qk(end - 1, NT - 1, NT - 1)
                move_q(end - 2, NT - 2)
                move_q(end - 1, NT - 1)
                wait(dve, s_qs, b * NT + NT)
                dve.tensor_reduce(qmx[:, :], qn2[:, :, :].rearrange("p t h -> p h t"), AX.X, ALU.max).then_inc(s_mxD, 1)
                wait(dve, s_mxT, b + 1)
                dve.tensor_reduce(qmT[:, :], bank(0)[0:H, 0:P], AX.X, ALU.max).then_inc(s_mxD, 1)
                wait(dve, s_mxD, 3 * b + 2)
                dve.tensor_scalar(qmD[:, :], ident[0:H, 0:H], qmT[:, 0:1], None, ALU.mult).then_inc(s_mxD, 1)
                wait(dve, s_mx, b + 1)
                dve.tensor_scalar(nbias[:, :], nm[:, 0:H], CESC, None, ALU.mult).then_inc(s_nb, 1)
                wait(dve, s_nb, 2 * b + 1)
                dve.tensor_scalar(nbias[:, :], nbias[:, :], -KSCALE * math.sqrt(DH), TOP, ALU.mult, ALU.add).then_inc(s_nb, 1)

                def parts(hh, h, k):
                    s = hh * STEPS + k
                    if not (isinstance(h, int) and k < NEP):
                        wait(dve, s_PV, s - NEP + 1)
                    if k in ACT_H:
                        wait(dve, s_EhA, hh * len(ACT_H) + act_h(k) + 1)
                    else:
                        wait(dve, s_E, s + 1)
                        dve.tensor_copy(e_h[:, k % NEP, :], e_f[:, k % NEF, :]).then_inc(s_EhD, 1)
                        wait(dve, s_EhD, hh * (STEPS - len(ACT_H)) + k - act_h(k) + 1)
                    dve.tensor_tensor(e_l[:, k % NEP, :], e_f[:, k % NEF, :], e_h[:, k % NEP, :], ALU.subtract).then_inc(s_El, 1)

                def move_out(unit):
                    wait(dve, s_PV, unit * NT + NT)
                    wait(dve, s_sum, unit)
                    for i in range(2):
                        dve.tensor_copy(ov[:, i * QT // 2:(i + 1) * QT // 2, :].rearrange("p (b q) c -> p b q c", q=2),
                                        ps_O[:, 2 * i:2 * i + 2, :, :]).then_inc(s_Oev, 1)

                def factors(unit, local):
                    wait(dve, s_sum, unit + 1)
                    r = rl[:, local * QT:local * QT + QT] if isinstance(local, int) else rl[:, bass.ds(local * QT, QT)]
                    l = lsum[:, local * QT:local * QT + QT] if isinstance(local, int) else lsum[:, bass.ds(local * QT, QT)]
                    dve.reciprocal(r, l).then_inc(s_rl, 1)
                    wait(dve, s_rl, 2 * unit + 1)
                    dve.tensor_scalar(r, r, CIV, None, ALU.mult).then_inc(s_rl, 1)

                def head_dve(b, h):
                    hh = b * H + h
                    for k in range(STEPS):
                        if k % NT == 1 and not (isinstance(h, int) and k < NT):
                            move_out(hh * NQB + k // NT - 1)
                        if k % NT == NT // 2 and not (isinstance(h, int) and k < NT):
                            factors(hh * NQB + k // NT - 1, h * NQB + k // NT - 1)
                        parts(hh, h, k)

                head_dve(b, 0)
                with dve.Fori(1, H) as h:
                    head_dve(b, h)

                front = Chain(dve, s_c, 2 * (2 * TG + 1))
                last5 = Chain(dve, s_c5, 2 * TG + 1)
                y = y_f[:, :, :].rearrange("p k (t d) -> p (k t) d", d=D)

                def x_tile(gi, t):
                    return x_all[:, gi * TG + t, :]

                def xe_tile(gi, t):
                    return xe[:, gi * TG + t, :]

                def low_attention(g, gi):
                    wait(dve, s_ah, g + 1)
                    hi, lo = splits[gi % 2]
                    dve.tensor_tensor(lo[:, :, :], ps_T3[gi], hi[:, :, :].bitcast(f32), ALU.subtract).then_inc(s_al, 1)

                def variances(src, before=lambda t: None):
                    for t in range(TG):
                        before(t)
                        front.link(dve.bn_stats(st[:, t, :], src(t)))
                    front.follow()
                    dve.sem_inc(s_held, 1)
                    for t in range(TG):
                        front.link(dve.bn_aggr(mv[:, t, :], st[:, t, :]))
                    front.follow()
                    dve.tensor_scalar(var[:, :], mv[:, :, 1], LN_EPS, None, ALU.add).then_inc(s_var3, 1)

                def projected(g, gi):
                    front.begin(g)
                    wait(dve, s_xa, 2 * g)

                    def two_tiles(t):
                        if t % 2 == 0:
                            wait(dve, s_Y, 2 * g + t // 2 + 1)
                            dve.tensor_tensor(y[:, t:t + 2, :], ps_Y[gi][t // 2].rearrange("p (t d) -> p t d", d=D),
                                              spread(bo_row[:, :], 1, 2), ALU.add).then_inc(s_yb, 1)
                            wait(dve, s_yb, 2 * g + t // 2 + 1)
                    variances(lambda t: y[:, t, :], two_tiles)

                def normal_y(g):
                    wait(dve, s_sd3, 2 * g + 1)
                    front.link(dve.reciprocal(rs[:, :], sd[:, :]))
                    front.follow()
                    for t in range(TG):
                        dve.tensor_scalar(y[:, t, :], y[:, t, :], mv[:, t, 0:1], rs[:, t:t + 1], ALU.subtract,
                                          ALU.mult).then_inc(s_yn, 1)

                def second_stats(g, gi):
                    wait(dve, s_yn, g * TG + TG)
                    variances(lambda t: x_tile(gi, t), lambda t: wait(dve, s_xa, 2 * g + t // 2 + 1))

                def normal_x(g, gi):
                    wait(dve, s_sd3, 2 * g + 2)
                    front.link(dve.reciprocal(rs[:, :], sd[:, :]))
                    front.follow()
                    for t in range(TG):
                        dve.tensor_scalar(xe_tile(gi, t), x_tile(gi, t), mv[:, t, 0:1], rs[:, t:t + 1], ALU.subtract,
                                          ALU.mult).then_inc(s_xn, 1)

                def low_n(g, gi):
                    wait(dve, s_nh, g + 1)
                    hi, lo = splits[gi % 2]
                    dve.tensor_tensor(lo[:, :, :], ps_T, hi[:, :, :].bitcast(f32), ALU.subtract).then_inc(s_nl, 1)

                def choose(g):
                    own = Chain(dve, s_Gr, GATE)
                    own.begin(g)
                    bc = lambda a: spread(a, 2, NE)
                    rk = spread(rank[:, :], 1, TG)
                    wait(dve, s_G, g + 1)
                    wait(dve, s_Xr, g * TG * NX)
                    wait(dve, s_XA, g * TG * NA)
                    own.link(dve.tensor_copy(gs[:, :, :], ps_G.rearrange("p (t e) -> p t e", e=NE)))
                    own.follow()
                    own.link(dve.tensor_reduce(gm[:, :], gs[:, :, :], AX.X, ALU.max))
                    own.follow()
                    own.link(dve.tensor_tensor(hot[:, :, :], gs[:, :, :], bc(gm[:, :]), ALU.is_equal))
                    own.follow()
                    own.link(dve.tensor_tensor(hot[:, :, :], hot[:, :, :], rk, ALU.mult))
                    own.follow()
                    own.link(dve.tensor_reduce(gm[:, :], hot[:, :, :], AX.X, ALU.max))
                    own.follow()
                    own.link(dve.tensor_tensor(hot[:, :, :], rk, bc(gm[:, :]), ALU.is_equal))
                    own.follow()
                    assert own.n == GATE

                ONTO_B = BY_DVE[2::2]

                def select(g, gi, t, experts=BY_DVE):
                    n = g * TG + t
                    for e in experts:
                        i = BY_DVE.index(e)
                        wait(dve, s_X, n * XR + e // 2 + 1)
                        if i == 0 and t == 0:
                            wait(dve, s_T4, g + 1)
                        same = [o for o in BY_DVE[:i] if (o in ONTO_B) == (e in ONTO_B)]
                        if same:
                            wait(dve, s_Xr, n * NX + BY_DVE.index(same[-1]) + 1)
                        elif e in ONTO_B:
                            wait(dve, s_XA, n * NA + NA)
                        a = f_b[:, t % 2, :] if e in ONTO_B else xe_tile(gi, t)
                        dve.scalar_tensor_tensor(out=a, in0=ps_X[e // 2][:, (e % 2) * D:(e % 2) * D + D],
                                                 scalar=hot[:, t, e:e + 1], in1=a, op0=ALU.mult, op1=ALU.add).then_inc(s_Xr, 1)

                def sum_stats(g, gi, t):
                    wait(dve, s_fs, g * TG + t + 1)
                    if t == 0:
                        last5.begin(g)
                    last5.link(dve.bn_stats(st5[:, t, :], xe_tile(gi, t)))

                def sum_variances(g):
                    last5.follow()
                    dve.sem_inc(s_held, 1)
                    for t in range(TG):
                        last5.link(dve.bn_aggr(mv5[:, t, :], st5[:, t, :]))
                    last5.follow()
                    dve.tensor_scalar(var5[:, :], mv5[:, :, 1], LN_EPS, None, ALU.add).then_inc(s_var5, 1)

                def sum_factors(g):
                    wait(dve, s_sd5, g + 1)
                    last5.begin(g, 2 * TG)
                    wait(dve, s_f5, g * TG)
                    last5.link(dve.reciprocal(rs5[:, :], sd5[:, :]))
                    last5.follow()
                    dve.scalar_tensor_tensor(out=nb5[:, :], in0=mv5[:, :, 0], scalar=-1.0, in1=rs5[:, :], op0=ALU.mult,
                                             op1=ALU.mult).then_inc(s_nb5, 1)

                g0 = b * NG
                low_attention(g0, 0)
                move_out(b * H * NQB + H * NQB - 1)
                projected(g0, 0)
                normal_y(g0)
                factors(b * H * NQB + H * NQB - 1, H * NQB - 1)
                low_attention(g0 + 1, 1)
                second_stats(g0, 0)
                normal_x(g0, 0)
                low_n(g0, 0)
                for gi in range(NG):
                    g, more = g0 + gi, gi + 1 < NG
                    if more and gi:
                        low_attention(g + 1, gi + 1)
                    choose(g)
                    select(g, gi, 0, BY_DVE[:2])
                    if more:
                        projected(g + 1, gi + 1)
                    select(g, gi, 0, BY_DVE[2:])
                    if more:
                        normal_y(g + 1)
                    if gi:
                        last5.begin(g - 1, TG - 1)
                        sum_stats(g - 1, gi - 1, TG - 1)
                        sum_variances(g - 1)
                    select(g, gi, 1)
                    if gi:
                        sum_factors(g - 1)
                    if more:
                        second_stats(g + 1, gi + 1)
                    sum_stats(g, gi, 0)
                    select(g, gi, 2, BY_DVE[:2])
                    if more:
                        normal_x(g + 1, gi + 1)
                    select(g, gi, 2, BY_DVE[2:])
                    sum_stats(g, gi, 1)
                    select(g, gi, 3, BY_DVE[:2])
                    if more:
                        low_n(g + 1, gi + 1)
                    select(g, gi, 3, BY_DVE[2:])
                    sum_stats(g, gi, 2)
                last5.begin(g0 + NG - 1, TG - 1)
                sum_stats(g0 + NG - 1, NG - 1, TG - 1)
                sum_variances(g0 + NG - 1)
                sum_factors(g0 + NG - 1)

        @block.tensor
        def _(pe):
            start_up(pe, "pe")

            def products(dst, terms):
                n = len(terms)
                for i, (l, r) in enumerate(terms):
                    ins = pe.matmul(dst, l, r, start=(i == 0), stop=(i == n - 1))
                return ins

            wait(pe, s_ones, 1)
            wait(pe, s_prepA, 2)
            pe.matmul(bank(0)[:, 0:1], ones[:, :], part[:, 0:1], start=True, stop=True).then_inc(s_prepP, 1)
            wait(pe, s_id, 4)
            wait(pe, s_prep, 3)
            wait(pe, s_ws, 1)

            def transpose_group(g, done):
                for k in range(KH):
                    for t in range(TG):
                        ins = pe.transpose(ps_T[:, k, t * P:(t + 1) * P], xhat[:, t, k * P:(k + 1) * P], ident[:, :])
                ins.then_inc(done, 1)

            def three(t, w_h, w_l, c0, c1, a_h=y_h, a_l=y_l):
                tok = slice(t * P, (t + 1) * P)
                return [(a[:, k, tok], w[:, k, c0:c1]) for a, w in ((a_h, w_h), (a_l, w_h), (a_h, w_l)) for k in range(KH)]

            def project(n, t):
                wait(pe, s_qkn, n - 1)
                wait(pe, s_vl, n - 1)
                products(ps_QK[t % 2], three(t % TG, wqkv_h, wqkv_l, 0, 2 * D))
                products(ps_V[t % 2], three(t % TG, wqkv_h, wqkv_l, 2 * D, 3 * D)).then_inc(s_P, 1)

            def transpose_qk(n, t):
                qs = qk_s[t % 2]
                wait(pe, s_lo, n + 1)
                wait(pe, s_qe, n)
                wait(pe, s_ke, n)
                for h in range(H):
                    pe.transpose(ps_TQ[:, h * P:(h + 1) * P], qs[:, h, 0:2 * DH], ident16[:, :])
                for h in range(H):
                    for a in range(2):
                        ins = pe.transpose(ps_TK[:, (2 * h + a) * P:(2 * h + a + 1) * P],
                                           qs[:, H + h, a * DH:(a + 2) * DH], ident16[:, :])
                ins.then_inc(s_T2, 1)

            with pe.Fori(0, NB) as b:
                def group_T(g):
                    wait(pe, s_xh, g * TG + TG)
                    wait(pe, s_yh, KH * g)
                    transpose_group(g, s_T)

                def a_pe(gi, first=False, last=False):
                    g = b * NG + gi
                    for t in range(TG):
                        n = g * TG + t
                        if t < TG - 1 or not last:
                            if t == TG - 1:
                                wait(pe, s_ys, g + 2)
                            project(n + 1, t + 1)
                        if t == 1 and not last:
                            group_T(g + 1)
                        if not (first and t < 1):
                            transpose_qk(n - 1, t - 1)

                wait(pe, s_E, b * H * STEPS)
                group_T(b * NG)
                wait(pe, s_ys, b * NG + 1)
                project(b * NT, 0)
                groups(pe, a_pe)
                transpose_qk(b * NT + NT - 1, NT - 1)
                wait(pe, s_mxD, 3 * b + 1)
                pe.transpose(bank(0)[0:H, 0:P], qmx[:, :], ident[:, :]).then_inc(s_mxT, 1)
                wait(pe, s_mxD, 3 * b + 3)
                pe.matmul(bank(0)[:, 0:H], ones[0:H, :], qmD[:, :], start=True, stop=True).then_inc(s_mxB, 1)
                wait(pe, s_mx, b + 1)
                wait(pe, s_ke, b * NT + NT)
                wait(pe, s_qe, b * NT + NT)

                def scores(hh, h, k):
                    s = hh * STEPS + k
                    qb, j = k // NT, k % NT
                    first = isinstance(h, int)
                    if not (first and k < 2):
                        wait(pe, s_E, s - 1)
                    nc.disable_value_cache = False
                    for a in range(2):
                        if first:
                            kt = k_T[:, a, h * N + j * P:h * N + (j + 1) * P]
                        else:
                            kt = k_T[:, a, bass.ds(h * N + j * P, P)]
                        for c in range(QB // BANK):
                            at = qb * QB + c * BANK
                            qt = q_T[:, h * N + at:h * N + at + BANK] if first else q_T[:, bass.ds(h * N + at, BANK)]
                            ins = pe.matmul(ps_S[k % 2][:, c * BANK:(c + 1) * BANK], kt, qt, start=(a == 0), stop=(a == 1),
                                            skip_group_check=True)
                    nc.disable_value_cache = True
                    ins.then_inc(s_S, 1)

                def pv(hh, h, k, unit):
                    s = hh * STEPS + k
                    j = k % NT
                    wait(pe, s_El, s + 1)
                    at = j * H + h
                    v = (lambda w: v_mm[:, at, 0:w]) if isinstance(at, int) else (
                        lambda w: v_mm[:, bass.ds(at, 1), 0:w].rearrange("p o w -> p (o w)"))
                    nc.disable_value_cache = False
                    for q in range(QT):
                        if j == 0 and q % (QT // 2) == 0:
                            wait(pe, s_Oev, 2 * unit - 1 + q // (QT // 2))
                        for e, w in ((e_h, VW), (e_l, DH + 1)):
                            ins = pe.matmul(ps_O[:, q // 2, q % 2, 0:w], e[:, k % NEP, q * P:(q + 1) * P], v(w),
                                            start=(j == 0 and q % 2 == 0 and w == VW), stop=(j == NT - 1 and w != VW),
                                            skip_group_check=True)
                    nc.disable_value_cache = True
                    ins.then_inc(s_PV, 1)

                def head_pe(b, h):
                    hh = b * H + h
                    for k in range(STEPS):
                        scores(hh, h, k)
                        for i in {LAG - 2: (k - LAG, k - LAG + 1), LAG - 1: ()}.get(k % NT, (k - LAG,)):
                            if i >= 0:
                                pv(hh, h, i, hh * NQB + i // NT)
                            elif not isinstance(h, int):
                                pv(hh - 1, h - 1, STEPS + i, hh * NQB - 1)

                head_pe(b, 0)
                with pe.Fori(1, H) as h:
                    head_pe(b, h)
                wait(pe, s_wf, 4)
                def attention_T(g, gi):
                    wait(pe, s_at, g + 1)
                    wait(pe, s_yb, 2 * g)
                    for k in range(KH):
                        for t in range(TG):
                            ins = pe.transpose(ps_T3[gi][:, k, t * P:(t + 1) * P], xa[:, t, k * P:(k + 1) * P], ident[:, :])
                    ins.then_inc(s_T3, 1)

                def project_attention(g, gi):
                    wait(pe, s_al, g + 1)
                    for i in range(2):
                        for t in range(2 * i, 2 * i + 2):
                            ins = products(ps_Y[gi][i][:, (t % 2) * D:(t % 2 + 1) * D],
                                           three(t, wo_h, wo_l, 0, D, *splits[gi % 2]))
                        ins.then_inc(s_Y, 1)

                def norm_T(g, gi):
                    wait(pe, s_xn, g * TG + TG)
                    wait(pe, s_Gr, g * GATE)
                    for k in range(KH):
                        for t in range(TG):
                            ins = pe.transpose(ps_T[:, k, t * P:(t + 1) * P], xe[:, gi * TG + t, k * P:(k + 1) * P], ident[:, :])
                    ins.then_inc(s_T4, 1)

                def gate(g, gi):
                    hi, lo = splits[gi % 2]
                    wait(pe, s_nl, g + 1)
                    products(ps_GT, [(w[:, k, :], a[:, k, :]) for a, w in ((hi, wg_h), (lo, wg_h), (hi, wg_l))
                                     for k in range(KH)]).then_inc(s_GT, 1)

                def gate_T(g):
                    wait(pe, s_gT, g + 1)
                    for t in range(TG):
                        ins = pe.matmul(ps_G[:, t * NE:(t + 1) * NE], g_T[:, t * P:(t + 1) * P], ident[0:NE, 0:NE],
                                        start=True, stop=True)
                    ins.then_inc(s_G, 1)

                def experts(g, gi, t, chunks):
                    n = g * TG + t
                    for c in chunks:
                        pair = (2 * c, 2 * c + 1)
                        if pair == BY_ACT:
                            wait(pe, s_XA, (n - 1) * NA + NA)
                        else:
                            wait(pe, s_Xr, (n - 1) * NX + 1 + BY_DVE.index(pair[1]))
                        products(ps_X[c], three(t, we_h, we_l, c * BANK, (c + 1) * BANK, *splits[gi % 2])).then_inc(s_X, 1)

                g0 = b * NG
                wait(pe, s_E, (b * H + H) * STEPS - 1)
                attention_T(g0, 0)
                for k in range(STEPS - LAG, STEPS):
                    pv(b * H + H - 1, H - 1, k, b * H * NQB + H * NQB - 1)

                wait(pe, s_E, (b * H + H) * STEPS)
                project_attention(g0, 0)
                wait(pe, s_Oev, 2 * (b * H * NQB + H * NQB))
                attention_T(g0 + 1, 1)
                norm_T(g0, 0)
                for gi in range(NG):
                    g, more = g0 + gi, gi + 1 < NG
                    gate(g, gi)
                    experts(g, gi, 0, range(1))
                    gate_T(g)
                    experts(g, gi, 0, range(1, 2))
                    if more:
                        project_attention(g + 1, gi + 1)
                    experts(g, gi, 0, range(2, XR))
                    for t in (1, 2):
                        experts(g, gi, t, range(XR))
                    experts(g, gi, 3, range(2))
                    if more:
                        norm_T(g + 1, gi + 1)
                    experts(g, gi, 3, range(2, XR))
                    if gi + 2 < NG:
                        attention_T(g + 2, gi + 2)


def kernel(**inputs):
    import numpy as np
    import concourse.bacc as bacc
    from concourse.bass_utils import run_bass_kernel_spmd

    def get(name):
        return np.asarray(inputs[name])

    we = get("L0_ffn_expert_w")
    arrays = {
        "x": get("L0_attn_x"),
        "wqkvT": np.concatenate([get("L0_attn_w_" + n).T for n in "qkv"], axis=1),
        "woT": get("L0_attn_w_o").T,
        "weT": we.transpose(2, 0, 1).reshape(we.shape[2], -1),
        "wgT": get("L0_ffn_gate_w").T,
        "ln_gamma": get("L0_attn_ln_gamma"),
        "ln_beta": get("L0_attn_ln_beta"),
        "q_gamma": get("L0_attn_q_gamma"),
        "k_gamma": get("L0_attn_k_gamma"),
        "b_o": get("L0_attn_b_o"),
    }
    arrays = {n: np.ascontiguousarray(a) for n, a in arrays.items()}
    nc = bacc.Bacc("TRN2", target_bir_lowering=False, num_devices=1)
    args = [nc.dram_tensor(n, a.shape, mybir.dt.from_np(a.dtype), kind="ExternalInput").ap() for n, a in arrays.items()]
    x = arrays["x"]
    out = nc.dram_tensor("out", x.shape, mybir.dt.from_np(x.dtype), kind="ExternalOutput").ap()
    build(nc, *args, out)
    return run_bass_kernel_spmd(nc, [arrays], core_ids=[0]).results[0]["out"]
```
